# Optimizing a Trainium2 kernel written in Bass

```python
import numpy as np
import jax
import jax.numpy as jnp

def _softmax(x, axis=-1):
    return jax.nn.softmax(x, axis=axis)

def _gelu(x):
    return jax.nn.gelu(x, approximate=True)

def _silu(x):
    return jax.nn.silu(x)

def _sigmoid(x):
    return jax.nn.sigmoid(x)

def _layernorm(x, axis=-1, eps=1e-05):
    m = jnp.mean(x, axis=axis, keepdims=True)
    v = jnp.var(x, axis=axis, keepdims=True)
    return (x - m) / jnp.sqrt(v + eps)

def _scatter_add(tgt, idx, src, axis=0):
    return tgt.at[idx].add(src)

def _segment_sum(src, seg, n):
    return jax.ops.segment_sum(src, seg, n)
kernel_name = 'mk_flamingo_gated_d1_seqx_r8_ab13e3'

def setup_inputs(seed: int=0):
    np.random.seed(seed)
    _w = jnp.asarray

    def _rec_inputs():
        import jax
        import jax.numpy as jnp
        _rk = jax.random.key(seed)
        x = 0.0002417 + 0.9998 * jax.random.normal(jax.random.fold_in(_rk, 1), (16, 64, 128), jnp.float32)
        _lenS = 64 - jax.random.randint(jax.random.fold_in(_rk, 7), (16,), 0, max(1, 64 // 4) + 1, jnp.int32)
        _lenS2 = 64 - jax.random.randint(jax.random.fold_in(_rk, 8), (16,), 0, max(1, 64 // 4) + 1, jnp.int32)
        _ctx_1024P = jax.random.normal(jax.random.fold_in(_rk, 11), (16, 16, 128), jnp.float32)
        _ctx_1024c = jax.random.dirichlet(jax.random.fold_in(_rk, 511), 0.3 * jnp.ones((16,), jnp.float32), (16, 64))
        _ctx_1024t = jnp.einsum('bsk,bkd->bsd', _ctx_1024c, _ctx_1024P)
        _ctx_1024t = _ctx_1024t * jax.lax.rsqrt(jnp.mean(jnp.square(_ctx_1024t)) + 1e-12) * 0.953939
        ctx_1024 = 7.22013e-05 + 1.00017 * (_ctx_1024t + 0.3 * jax.random.normal(jax.random.fold_in(_rk, 611), (16, 64, 128), jnp.float32))
        _g = jax.random.normal(jax.random.fold_in(_rk, 9001), (2, 1), jnp.float32)
        _g = jnp.sign(_g) * jnp.maximum(jnp.abs(_g), 1.0) + (_g == 0) * 1.0
        g_xattn = _g[0]
        g_ffn = _g[1]
        return (x, ctx_1024, g_xattn, g_ffn)
    x, ctx_1024, g_xattn, g_ffn = _rec_inputs()

    def _L0_xattn_setup():
        import jax, jax.numpy as jnp
        import numpy as np
        D_MODEL = 128
        B, S = (4, 256)
        key = jax.random.key(seed)
        ks = jax.random.split(key, 10)
        s = 1.0 / np.sqrt(D_MODEL)
        return {'k': jax.random.normal(ks[0], (B, S, D_MODEL), jnp.float32), 'v': jax.random.normal(ks[1], (B, S, D_MODEL), jnp.float32), 'q': jax.random.normal(ks[2], (B, S, D_MODEL), jnp.float32), 'Wk': jax.random.normal(ks[3], (D_MODEL, D_MODEL), jnp.float32) * s, 'Wv': jax.random.normal(ks[4], (D_MODEL, D_MODEL), jnp.float32) * s, 'bv': jnp.zeros((D_MODEL,), jnp.float32), 'Wq': jax.random.normal(ks[5], (D_MODEL, D_MODEL), jnp.float32) * s, 'bq': jnp.zeros((D_MODEL,), jnp.float32), 'Wo': jax.random.normal(ks[6], (D_MODEL, D_MODEL), jnp.float32) * s, 'bo': jnp.zeros((D_MODEL,), jnp.float32)}
    _L0_xattn_all = _L0_xattn_setup()
    _L0_xattn_in = {k: v for k, v in _L0_xattn_all.items() if k in ('Wk', 'Wv', 'bv', 'Wq', 'bq', 'Wo', 'bo')}
    del _L0_xattn_all

    def _L0_ffn_setup():
        import jax, jax.numpy as jnp
        import numpy as np
        NUM_EXPERTS = 8
        TOP_K = 2
        key = jax.random.key(seed)
        ks = jax.random.split(key, 6)
        B, S, D, F = (2, 256, 128, 512)
        E = NUM_EXPERTS
        sd = 1.0 / np.sqrt(D)
        sf = 1.0 / np.sqrt(F)
        return {'x': jax.random.normal(ks[0], (B, S, D), dtype=jnp.float32), 'gate_w': jax.random.normal(ks[1], (E, D), dtype=jnp.float32) * sd, 'w1': jax.random.uniform(ks[2], (F, E, D), dtype=jnp.float32, minval=-sd, maxval=sd), 'b1': jax.random.uniform(ks[3], (E, F), dtype=jnp.float32, minval=-sd, maxval=sd), 'w2': jax.random.uniform(ks[4], (D, E, F), dtype=jnp.float32, minval=-sf, maxval=sf), 'b2': jax.random.uniform(ks[5], (E, D), dtype=jnp.float32, minval=-sf, maxval=sf)}
    _L0_ffn_all = _L0_ffn_setup()
    _L0_ffn_in = {k: v for k, v in _L0_ffn_all.items() if k in ('gate_w', 'w1', 'b1', 'w2', 'b2')}
    del _L0_ffn_all
    return {'x': x, 'ctx_1024': ctx_1024, 'g_xattn': g_xattn, 'g_ffn': g_ffn, 'L0_xattn_Wk': _L0_xattn_in['Wk'], 'L0_xattn_Wv': _L0_xattn_in['Wv'], 'L0_xattn_bv': _L0_xattn_in['bv'], 'L0_xattn_Wq': _L0_xattn_in['Wq'], 'L0_xattn_bq': _L0_xattn_in['bq'], 'L0_xattn_Wo': _L0_xattn_in['Wo'], 'L0_xattn_bo': _L0_xattn_in['bo'], 'L0_ffn_gate_w': _L0_ffn_in['gate_w'], 'L0_ffn_w1': _L0_ffn_in['w1'], 'L0_ffn_b1': _L0_ffn_in['b1'], 'L0_ffn_w2': _L0_ffn_in['w2'], 'L0_ffn_b2': _L0_ffn_in['b2']}

def reference(x, ctx_1024, g_xattn, g_ffn, L0_xattn_Wk, L0_xattn_Wv, L0_xattn_bv, L0_xattn_Wq, L0_xattn_bq, L0_xattn_Wo, L0_xattn_bo, L0_ffn_gate_w, L0_ffn_w1, L0_ffn_b1, L0_ffn_w2, L0_ffn_b2):
    import jax
    import jax.numpy as jnp

    def _L0_xattn_ref(k, v, q, Wk, Wv, bv, Wq, bq, Wo, bo):
        import jax, jax.numpy as jnp
        import numpy as np
        D_MODEL = 128
        B, S = (4, 256)
        kp = jnp.einsum('bsd,ed->bse', k, Wk)
        vp = jnp.einsum('bsd,ed->bse', v, Wv) + bv
        qp = jnp.einsum('bsd,ed->bse', q, Wq) + bq
        scale = 1.0 / jnp.sqrt(jnp.float32(kp.shape[-1]))
        scores = jnp.einsum('bqd,bkd->bqk', qp, kp) * scale
        probs = jax.nn.softmax(scores, axis=-1)
        ctx = jnp.einsum('bqk,bkd->bqd', probs, vp)
        return jnp.einsum('bqd,ed->bqe', ctx, Wo) + bo

    def _L0_ffn_ref(x, gate_w, w1, b1, w2, b2):
        import jax, jax.numpy as jnp
        import numpy as np
        NUM_EXPERTS = 8
        TOP_K = 2
        logits = jnp.einsum('bsd,ed->bse', x, gate_w)
        probs = jax.nn.softmax(logits, axis=-1)
        topk_probs, topk_idx = jax.lax.top_k(probs, TOP_K)
        oh = jax.nn.one_hot(topk_idx, NUM_EXPERTS, dtype=x.dtype)
        h = jnp.einsum('bsd,fed,bske->bskf', x, w1, oh)
        h = h + jnp.take(b1, topk_idx, axis=0)
        h = jax.nn.gelu(h)
        y = jnp.einsum('bskf,def,bske->bskd', h, w2, oh)
        y = y + jnp.take(b2, topk_idx, axis=0)
        out = jnp.sum(y * topk_probs[..., None], axis=-2)
        return out
    x = x + jnp.tanh(g_xattn[0]) * _L0_xattn_ref(ctx_1024, ctx_1024, _layernorm(x, axis=-1), L0_xattn_Wk, L0_xattn_Wv, L0_xattn_bv, L0_xattn_Wq, L0_xattn_bq, L0_xattn_Wo, L0_xattn_bo)
    x = x + jnp.tanh(g_ffn[0]) * _L0_ffn_ref(_layernorm(x, axis=-1), L0_ffn_gate_w, L0_ffn_w1, L0_ffn_b1, L0_ffn_w2, L0_ffn_b2)
    return x

_drawn_inputs = setup_inputs


def setup_inputs(seed=0):
    import zlib

    import numpy as np

    out = dict(_drawn_inputs(seed))
    spreads = {'L0_xattn_bv': (0.0, 0.1), 'L0_xattn_bq': (0.0, 0.39), 'L0_xattn_bo': (0.0, 0.1)}
    factors = {'L0_ffn_b1': 7.97, 'L0_ffn_b2': 5.598}
    for name, (base, spread) in spreads.items():
        noise = np.random.default_rng([zlib.crc32(name.encode()), seed]).standard_normal(out[name].shape)
        drawn = base * np.exp(spread * noise) if base else spread * noise
        out[name] = jnp.asarray(drawn.astype(out[name].dtype))
    for name, factor in factors.items():
        out[name] = (out[name] * factor).astype(out[name].dtype)
    return out
```

```python
from contextlib import ExitStack

import concourse.bass as bass
from concourse import mybir

ALU = mybir.AluOpType
ACT = mybir.ActivationFunctionType
AX_X = mybir.AxisListType.X
F32, F16, BF16 = mybir.dt.float32, mybir.dt.float16, mybir.dt.bfloat16
I32, U32 = mybir.dt.int32, mybir.dt.uint32

P = 128
BATCH, SEQ = 16, 64
TOKENS = BATCH * SEQ
TILES = TOKENS // P
GROUP = 2
GROUPS = TILES // GROUP
EXPERTS, TOP_K, FF = 8, 2, 512
BLOCKS = FF // P
SLOTS = TOP_K * TOKENS
HALVES = 2
SLOT_TILE = HALVES * P
EDGES = TOKENS // SLOT_TILE
REGION = TOKENS + SLOT_TILE
RUNS = P // EXPERTS
PAD_RUN = SLOT_TILE // RUNS
PAD_ROW = EXPERTS * REGION
N_TILES = (SLOTS - EXPERTS) // SLOT_TILE + EXPERTS
ROW = P + 2
TARGET, GATE = P, P + 1
NO_TARGET = 4 * SLOTS
EPS = 1e-5
WSCALE = 16.0
SCORE_SCALE = float(P) ** -0.5
(SCORES, MAXIMUM, EXPONENT, PROBS_T, COPY_PROBS_T, ATTEND, RESIDUAL, RSTD2, NORM2, NORM2_T, COPY_NORM2_T, ROUTE,
 CHOOSE, RANKS, FILL, SEND) = range(16)
SKEW = 4
STEPS = SKEW * (GROUPS - 1) + SEND + 1
WQ, WK, WV, WOT, GATEW, BQ, BV, BO, GX, GF, B1 = 0, P, 2 * P, 3 * P, 4 * P, 4 * P + 8, 4 * P + 9, 4 * P + 10, 5 * P + 10, 5 * P + 11, 5 * P + 12
WCOLS = B1 + EXPERTS * BLOCKS


def gated_block(nc, x, ctx_t, wpack, b2, w1, w2, out):
    ctx = ExitStack()
    with ctx:
        def sb(name, shape, dt):
            return ctx.enter_context(nc.sbuf_tensor(name, shape, dt))

        def sem(name):
            return ctx.enter_context(nc.semaphore(name))

        rows_dram = nc.dram_tensor("dispatched", [PAD_ROW + SLOT_TILE, ROW], I32, kind="Internal").ap()
        results_dram = nc.dram_tensor("results", [SLOTS, P], F32, kind="Internal").ap()

        ident = sb("ident", [P, P], F32)
        ident16 = sb("ident16", [P, P], F16)
        before = sb("before", [P, P], BF16)
        ones = sb("ones", [P, P], BF16)
        ones_col = sb("ones_col", [P, 1], F32)
        iota_i = sb("iota_i", [P, EXPERTS], I32)
        iota_e = sb("iota_e", [P, EXPERTS], F32)
        region_i = sb("region_i", [P, EXPERTS], I32)
        region = sb("region", [P, EXPERTS], F32)
        target = sb("target", [P, TILES, TOP_K], I32)
        pad_rows = sb("pad_rows", [P, PAD_RUN, ROW], I32)
        run_sel = sb("run_sel", [P, EXPERTS], F32)
        run_i = sb("run_i", [P, EXPERTS], I32)
        run_from = sb("run_from", [P, EXPERTS], F32)
        run_row = sb("run_row", [P, EXPERTS], F32)
        run_word = sb("run_word", [P, EXPERTS], F32)
        pad_at = sb("pad_at", [P, 1], F32)
        pad_slot = sb("pad_slot", [P, 1], U32)
        minus_half = sb("minus_half", [P, TILES], F32)
        out_sel = sb("out_sel", [33, P], F16)
        tile_i = sb("tile_i", [1, N_TILES, EXPERTS], I32)
        tile_no = sb("tile_no", [1, N_TILES, EXPERTS], F32)
        edge_i = sb("edge_i", [1, EXPERTS, EDGES], I32)
        edge = sb("edge", [1, EXPERTS, EDGES], F32)
        upto = sb("upto", [1, EXPERTS, EXPERTS], F32)

        x_sb = sb("x_sb", [P, TILES, P], F32)
        ctx_sb = sb("ctx_sb", [P, TOKENS], F32)
        wp = sb("wp", [P, WCOLS], F32)
        b2_in = sb("b2_in", [33, EXPERTS * P], F32)
        w1_sb = sb("w1_sb", [P, EXPERTS, FF], F32)
        w2_sb = sb("w2_sb", [P, EXPERTS, FF], F32)

        w1_hi = sb("w1_hi", [P, EXPERTS, FF], F16)
        w1_lo = sb("w1_lo", [P, EXPERTS, FF], F16)
        w2_hi = sb("w2_hi", [P, EXPERTS, FF], F16)
        w2_lo = sb("w2_lo", [P, EXPERTS, FF], F16)
        b2_hi = sb("b2_hi", [33, EXPERTS * P], F16)
        b2_16 = sb("b2_16", [33, EXPERTS, P], F16)

        fused = sb("fused", [P, 3 * P + 1], F32)
        tanhs = sb("tanhs", [P, 2], F32)
        out_bias = sb("out_bias", [P, P], F32)
        x_bias = sb("x_bias", [P, TILES, P], F32)
        stats = sb("stats", [P, TILES, 6], F32)
        meanvar = sb("meanvar", [P, TILES, 2], F32)
        var_eps = sb("var_eps", [P, TILES], F32)
        rstd = sb("rstd", [P, TILES], F32)
        xn = sb("xn", [P, TILES, P], F32)
        xn_t = sb("xn_t", [P, TOKENS], F32)
        q_t = sb("q_t", [P, TOKENS], F32)
        v_sb = sb("v_sb", [P, TOKENS], F32)
        s_max = sb("s_max", [P, GROUPS, GROUP], F32)
        s_sub = sb("s_sub", [P, GROUPS, GROUP, SEQ], F32)
        probs = sb("probs", [P, TILES, P], F32)
        p_t = sb("p_t", [P, GROUPS, GROUP * P], F32)
        rden = sb("rden", [P, GROUPS, GROUP], F32)
        rgate = sb("rgate", [P, GROUPS, GROUP], F32)
        x1 = sb("x1", [P, TILES, P], F32)

        stats2 = sb("stats2", [P, TILES, 6], F32)
        meanvar2 = sb("meanvar2", [P, TILES, 2], F32)
        var_eps2 = sb("var_eps2", [P, TILES], F32)
        rstd2 = sb("rstd2", [P, TILES], F32)
        xn2 = sb("xn2", [P, TILES, P], F32)
        xn2_t = sb("xn2_t", [P, GROUPS, GROUP * P], F32)
        logits = sb("logits", [P, TILES, EXPERTS], F32)
        sorted_l = sb("sorted_l", [P, TILES, EXPERTS], F32)
        index = sb("index", [P, TILES, EXPERTS], U32)
        index_f = sb("index_f", [P, TILES, TOP_K], F32)
        choice = sb("choice", [P, TILES, TOP_K, EXPERTS], F32)
        chosen = sb("chosen", [P, TILES, EXPERTS], BF16)
        shifted = sb("shifted", [P, TILES, EXPERTS], F32)
        exps = sb("exps", [P, TILES, EXPERTS], F32)
        exp_sum = sb("exp_sum", [P, TILES], F32)
        exp_rec = sb("exp_rec", [P, TILES], F32)
        gates = sb("gates", [P, TILES, TOP_K], F32)
        place = sb("place", [P, TILES, EXPERTS], F32)
        place_k = sb("place_k", [P, TILES, TOP_K, EXPERTS], F32)
        slot_f = sb("slot_f", [P, TILES, TOP_K], F32)
        slot = sb("slot", [P, TOP_K * TILES], U32)
        rows = sb("rows", [P, TILES, TOP_K, ROW], I32)

        counts = sb("counts", [1, EXPERTS], F32)
        over = sb("over", [1, EXPERTS, EDGES], F32)
        n_tiles = sb("n_tiles", [1, EXPERTS], F32)
        upto_n = sb("upto_n", [1, EXPERTS, EXPERTS], F32)
        ends = sb("ends", [1, EXPERTS], F32)
        past = sb("past", [1, N_TILES, EXPERTS], F32)
        past_n = sb("past_n", [1, N_TILES, EXPERTS], F32)
        tile_e = sb("tile_e", [1, N_TILES], F32)
        tile_base = sb("tile_base", [1, N_TILES], F32)
        tile_row = sb("tile_row", [1, N_TILES], F32)
        tile_row2 = sb("tile_row2", [1, N_TILES], F32)
        tile_rows = sb("tile_rows", [1, N_TILES], I32)
        tile_experts = sb("tile_experts", [1, N_TILES], I32)

        in_rows = sb("in_rows", [P, 2, HALVES, ROW], I32)
        xs_t = sb("xs_t", [P, 2, 2, SLOT_TILE], F16)
        hid = sb("hid", [P, 2, BLOCKS, SLOT_TILE], F32)
        hid_hi = sb("hid_hi", [P, 2, BLOCKS, SLOT_TILE], F16)
        hid_lo = sb("hid_lo", [P, 2, BLOCKS, SLOT_TILE], F16)
        y_sb = sb("y_sb", [P, 2, HALVES, P], F32)
        ahead = sb("ahead", [P, 2, HALVES, 2], I32)
        aims = sb("aims", [P, 2, HALVES, 2], I32)

        row_parts, in_parts = rows[:].bitcast(F16), in_rows[:].bitcast(F16)

        res = sb("res", [P, TOP_K, TILES, P], F32)
        out_sb = sb("out_sb", [P, TILES, P], F32)

        bank = [ctx.enter_context(nc.psum_tensor(f"bank{i}", [P, 512], F32)) for i in range(8)]
        once = bank[0]
        v_bank, xnt_bank, q_bank = [bank[1], bank[5]], [bank[2], bank[6]], [bank[3], bank[7]]
        turn = [bank[1], bank[5]]
        probs_bank = [bank[2], bank[6]]
        score = [bank[3], bank[7]]
        DEN, LOGIT, RANK, COUNT = 400, 408, 432, 456
        xs_ps = [bank[0], bank[4]]
        hid_ps = [[bank[1], bank[3]], [bank[5], bank[7]]]
        y_ps = [bank[2], bank[6]]

        ld_x, ld_ctx, ld_w = [sem(f"ld_x{i}") for i in range(2)], sem("ld_ctx"), sem("ld_w")
        ld_b, ld_w1, ld_w2 = sem("ld_b"), sem("ld_w1"), sem("ld_w2")
        pool_set, consts, dve_set = sem("pool_set"), sem("consts"), sem("dve_set")
        zeroed = sem("zeroed")
        fused_ps, fused_ok, tanh_ok = sem("fused_ps"), sem("fused_ok"), sem("tanh_ok")
        bias_ok, xbias_ok = sem("bias_ok"), sem("xbias_ok")
        dve = sem("dve")
        var_ok, rstd_ok, xn_ok = sem("var_ok"), sem("rstd_ok"), sem("xn_ok")
        v_ps, v_ok = sem("v_ps"), sem("v_ok")
        xnt_ps, xnt_ok, q_ps, q_ok = sem("xnt_ps"), sem("xnt_ok"), sem("q_ps"), sem("q_ok")
        s_ps, sub_ok, prob_ok = sem("s_ps"), sem("sub_ok"), sem("prob_ok")
        pt_ps, pt_ok, o_ps = sem("pt_ps"), sem("pt_ok"), sem("o_ps")
        var2_ok, rstd2_ok, xn2_ok = sem("var2_ok"), sem("rstd2_ok"), sem("xn2_ok")
        x2t_ps, x2t_ok, logit_ps = sem("x2t_ps"), sem("x2t_ok"), sem("logit_ps")
        chosen_ok, rank_ps, shift_ok, exps_ok = sem("chosen_ok"), sem("rank_ps"), sem("shift_ok"), sem("exps_ok")
        hi_ok, row_ok = sem("hi_ok"), sem("row_ok")
        group_done = sem("group_done")
        sent = sem("sent")
        padded, pads_ok, filled = sem("padded"), sem("pads_ok"), sem("filled")
        count_ps, table_ok = sem("count_ps"), sem("table_ok")
        w1hi_ok, w1_ok, w2hi_ok, w2_ok, b2_ok = sem("w1hi_ok"), sem("w1_ok"), sem("w2hi_ok"), sem("w2_ok"), sem("b2_ok")
        loaded = [sem(f"loaded{i}") for i in range(2)]
        xs_in_ps, xs_ok, hid_in_ps, hid_hi_ok, hid_ok, hid_lo_ok = sem("xs_in_ps"), sem("xs_ok"), sem("hid_in_ps"), sem("hid_hi_ok"), sem("hid_ok"), sem("hid_lo_ok")
        y_in_ps, y_ok, row_read, aim_ok = sem("y_in_ps"), sem("y_ok"), sem("row_read"), sem("aim_ok")
        may_scatter = sem("may_scatter")
        scattered = [sem(f"scattered{i}") for i in range(2)]
        ld_res, out_ok, stored = [sem(f"ld_res{i}") for i in range(4)], sem("out_ok"), sem("stored")

        x_view = x.rearrange("(t p) d -> p t d", p=P)
        out_view = out.rearrange("(t p) d -> p t d", p=P)
        res_view = results_dram.rearrange("(k t p) d -> p k t d", p=P, k=TOP_K)
        HALF = TILES // 2

        def experts_of(g):
            return slice(g * EXPERTS // GROUPS, (g + 1) * EXPERTS // GROUPS)

        def group(g):
            return slice(g * GROUP, (g + 1) * GROUP)

        block = ctx.enter_context(nc.Block())

        @block.sync
        def _(sp):
            for i in range(2):
                sp.dma_start(x_sb[:, i * HALF:(i + 1) * HALF, :], x_view[:, i * HALF:(i + 1) * HALF, :]).then_inc(ld_x[i], 16)
            sp.dma_start(ctx_sb[:], ctx_t).then_inc(ld_ctx, 16)
            sp.dma_start(w1_sb[:], w1).then_inc(ld_w1, 16)
            sp.wait_ge(zeroed, 1)
            for i in range(2):
                sp.dma_start(b2_in[32 * i:32 * i + 1, :], b2).then_inc(ld_b, 16)
            sp.dma_start(w2_sb[:], w2).then_inc(ld_w2, 16)
            sp.wait_ge(consts, 1)
            sp.dma_start(rows_dram[PAD_ROW:PAD_ROW + SLOT_TILE, :].rearrange("(p r) c -> p r c", r=HALVES), pad_rows[:, 0:HALVES, :]).then_inc(padded, 16)
            sp.wait_ge(sent, 16 * SLOTS // P)
            sp.wait_ge(filled, 16)
            sp.wait_ge(padded, 16)

            sp.wait_ge(table_ok, 1)

            def load_rows(t, s, first=False):
                at = sp.value_load(tile_rows[0:1, bass.ds(t, 1)], min_val=0, max_val=PAD_ROW)
                if not first:
                    sp.wait_ge(row_read, t - 1)
                sp.dma_start(in_rows[:, s, :, :], rows_dram[bass.ds(at, SLOT_TILE), :].rearrange("(p r) c -> p r c", r=HALVES)).then_inc(loaded[s], 16)

            load_rows(0, 0, True)
            load_rows(1, 1, True)
            with sp.Fori(1, N_TILES // 2) as k:
                load_rows(2 * k, 0)
                load_rows(2 * k + 1, 1)
            load_rows(N_TILES - 1, 0)
            sp.wait_ge(scattered[0], 16 * HALVES * ((N_TILES + 1) // 2))
            sp.wait_ge(scattered[1], 16 * HALVES * (N_TILES // 2))
            for i in range(4):
                q = slice(2 * i, 2 * i + 2)
                for k in range(TOP_K):
                    sp.dma_start(res[:, k, q, :], res_view[:, k, q, :]).then_inc(ld_res[i], 16)
            for i in range(4):
                q = slice(2 * i, 2 * i + 2)
                sp.wait_ge(out_ok, i + 1)
                sp.dma_start(out_view[:, q, :], out_sb[:, q, :]).then_inc(stored, 16)
            sp.wait_ge(stored, 64)

        def send(pool, g):
            pool.wait_ge(row_ok, g + 1)
            for t in range(g * GROUP, (g + 1) * GROUP):
                for k in range(TOP_K):
                    j = TOP_K * t + k
                    pool.indirect_dma_start(rows_dram, bass.IndirectOffsetOnAxis(ap=slot[:, j:j + 1], axis=0),
                                            rows[:, t, k, :], None).then_inc(sent, 16)

        @block.gpsimd
        def _(pool):
            for m in (ident, ident16, probs, out_sel):
                pool.memset(m[:], 0.0).then_inc(pool_set, 1)
            pool.memset(pad_rows[:], 0).then_inc(pool_set, 1)
            pool.memset(before[:], 1.0).then_inc(pool_set, 1)
            pool.memset(upto[:], 1.0).then_inc(pool_set, 1)
            pool.memset(minus_half[:], -0.5).then_inc(pool_set, 1)
            pool.iota(iota_i[:], [[1, EXPERTS]], base=0, channel_multiplier=0).then_inc(pool_set, 1)
            pool.iota(region_i[:], [[REGION, EXPERTS]], base=0, channel_multiplier=0).then_inc(pool_set, 1)
            pool.iota(target[:], [[P, TILES], [TOKENS, TOP_K]], base=0, channel_multiplier=1).then_inc(pool_set, 1)
            pool.iota(tile_i[:], [[1, N_TILES], [0, EXPERTS]], base=0, channel_multiplier=0).then_inc(pool_set, 1)
            pool.memset(run_sel[:], float(ROW)).then_inc(pool_set, 1)
            pool.iota(run_i[:], [[REGION - SLOT_TILE, EXPERTS]], base=0, channel_multiplier=PAD_RUN).then_inc(pool_set, 1)
            pool.iota(edge_i[:], [[0, EXPERTS], [SLOT_TILE, EDGES]], base=0, channel_multiplier=0).then_inc(pool_set, 1)
            pool.wait_ge(pool_set, 15)
            pool.affine_select(out=ident[:], in_=ident[:], compare_op=ALU.not_equal, fill=1.0, base=0,
                               pattern=[[-1, P]], channel_multiplier=1).then_inc(pool_set, 1)
            pool.affine_select(out=ident16[:], in_=ident16[:], compare_op=ALU.not_equal, fill=1.0, base=0,
                               pattern=[[-1, P]], channel_multiplier=1).then_inc(pool_set, 1)
            pool.affine_select(out=before[:], in_=before[:], compare_op=ALU.is_gt, fill=0.0, base=0,
                               pattern=[[1, P]], channel_multiplier=-1).then_inc(pool_set, 1)
            pool.affine_select(out=upto[:], in_=upto[:], compare_op=ALU.is_ge, fill=0.0, base=0,
                               pattern=[[1, EXPERTS], [-1, EXPERTS]], channel_multiplier=0).then_inc(pool_set, 1)
            pool.memset(pad_rows[:, :, TARGET:TARGET + 1], NO_TARGET).then_inc(pool_set, 1)
            pool.affine_select(out=run_sel[:], in_=run_sel[:], compare_op=ALU.is_ge, fill=0.0, base=0,
                               pattern=[[-RUNS, EXPERTS]], channel_multiplier=1).then_inc(pool_set, 1)
            for i in range(2):
                if i:
                    pool.wait_ge(pool_set, 22)
                pool.affine_select(out=out_sel[:], in_=out_sel[:], compare_op=ALU.not_equal, fill=1.0,
                                   base=-32 * i, pattern=[[0, P]], channel_multiplier=1).then_inc(pool_set, 1)
            pool.affine_select(out=run_sel[:], in_=run_sel[:], compare_op=ALU.is_ge, fill=0.0, base=RUNS - 1,
                               pattern=[[RUNS, EXPERTS]], channel_multiplier=-1).then_inc(pool_set, 1)
            pool.wait_ge(pool_set, 24)
            pool.memset(ones_col[:], 1.0).then_inc(consts, 1)

            for i in range(2):
                h = slice(i * HALF, (i + 1) * HALF)
                pool.wait_ge(var_ok, i + 1)
                pool.tensor_tensor(rstd[:, h], var_eps[:, h], minus_half[:, h], ALU.pow).then_inc(rstd_ok, 1)
            pool.wait_ge(bias_ok, 1)
            pool.tensor_tensor(x_bias[:], x_sb[:], out_bias[:, None, :].to_broadcast((P, TILES, P)), ALU.add).then_inc(xbias_ok, 1)
            def rstd_of(g):
                pool.wait_ge(var2_ok, g + 1)
                pool.tensor_tensor(rstd2[:, group(g)], var_eps2[:, group(g)], minus_half[:, group(g)], ALU.pow).then_inc(rstd2_ok, 1)

            for step in range(STEPS):
                for g in range(GROUPS):
                    stage = step - SKEW * g
                    if stage == RSTD2:
                        rstd_of(g)
                    elif stage == SEND:
                        send(pool, g)
            pool.wait_ge(pads_ok, 1)
            pool.indirect_dma_start(rows_dram.rearrange("s (c one) -> (s c) one", one=1),
                                    bass.IndirectOffsetOnAxis(ap=pad_slot[:], axis=0),
                                    pad_rows[:].rearrange("p r c -> p (r c)"), None).then_inc(filled, 16)

            limit = pool.to_reg(SLOTS - 1)

            def scatter(t, s):
                pool.wait_ge(y_ok, t + 1)
                pool.sem_inc(may_scatter, 1)
                for r in range(HALVES):
                    pool.indirect_dma_start(results_dram, bass.IndirectOffsetOnAxis(ap=aims[:].bitcast(U32)[:, s, r, 0:1], axis=0),
                                            y_sb[:, s, r, :], None, bounds_check=limit,
                                            oob_is_err=False).then_inc(scattered[s], 16)

            with pool.Fori(0, N_TILES // 2) as k:
                scatter(2 * k, 0)
                scatter(2 * k + 1, 1)
            scatter(N_TILES - 1, 0)

        @block.scalar
        def _(act):
            act.dma_start(wp[:], wpack).then_inc(ld_w, 16)
            act.wait_ge(ld_w, 16)
            act.activation(tanhs[:], wp[:, GX:GF + 1], ACT.Tanh).then_inc(tanh_ok, 1)
            act.wait_ge(fused_ps, 1)
            act.activation(fused[:], once[:, 0:3 * P + 1], ACT.Copy).then_inc(fused_ok, 1)

            def to_sbuf(at, psum, ready, copied, h, bias=None):
                act.wait_ge(ready, h + 1)
                act.activation(at[:, h * HALF * P:(h + 1) * HALF * P], psum[h][:, :], ACT.Copy if bias is None else ACT.Identity,
                               **({} if bias is None else {"bias": bias})).then_inc(copied, 1)

            for h in range(2):
                to_sbuf(xn_t, xnt_bank, xnt_ps, xnt_ok, h)
                to_sbuf(q_t, q_bank, q_ps, q_ok, h, bias=fused[:, 2 * P:2 * P + 1])
                to_sbuf(v_sb, v_bank, v_ps, v_ok, h)

            def exp_scores(g):
                act.wait_ge(sub_ok, g + 1)
                for h in range(2):
                    half = slice(h * SEQ, (h + 1) * SEQ)
                    act.activation(probs[half, group(g), half], s_sub[half, g, :, :], ACT.Exp,
                                   scale=SCORE_SCALE).then_inc(prob_ok, 1)

            def copy_pt(g):
                act.wait_ge(pt_ps, g + 1)
                act.activation(p_t[:, g, :], probs_bank[g % 2][:, 0:GROUP * P], ACT.Copy).then_inc(pt_ok, 1)

            def copy_x2t(g):
                act.wait_ge(x2t_ps, g + 1)
                act.activation(xn2_t[:, g, :], turn[g % 2][:, 0:GROUP * P], ACT.Copy).then_inc(x2t_ok, 1)

            def high_part(g):
                act.wait_ge(xn2_ok, g + 1)
                for k in range(TOP_K):
                    act.activation(row_parts[:, group(g), k, 0:P], xn2[:, group(g), :], ACT.Copy).then_inc(hi_ok, 1)

            def exp_logits(g):
                act.wait_ge(shift_ok, g + 1)
                act.activation(exps[:, group(g), :], shifted[:, group(g), :], ACT.Exp).then_inc(exps_ok, 1)

            def weights_hi(to, at, loaded_all, made, i):
                act.wait_ge(loaded_all, 16)
                q = experts_of(i)
                act.activation(to[:, q], at[:, q], ACT.Copy, scale=WSCALE).then_inc(made, 1)

            act.wait_ge(consts, 1)
            for step in range(STEPS):
                for g in range(GROUPS):
                    stage = step - SKEW * g
                    if stage == EXPONENT:
                        exp_scores(g)
                    elif stage == COPY_PROBS_T:
                        copy_pt(g)
                        weights_hi(w1_hi, w1_sb, ld_w1, w1hi_ok, g)
                    elif stage == COPY_NORM2_T:
                        copy_x2t(g)
                        high_part(g)
                    elif stage == RANKS:
                        exp_logits(g)
                        weights_hi(w2_hi, w2_sb, ld_w2, w2hi_ok, g)

            b1 = wp[:, B1:B1 + EXPERTS * BLOCKS].rearrange("p (e b) -> p e b", b=BLOCKS)

            def gelu(t, s, first=False):
                e = act.value_load(tile_experts[0:1, bass.ds(t, 1)], min_val=0, max_val=EXPERTS - 1)
                if not first:
                    act.wait_ge(y_in_ps, t - 1)
                for b in range(BLOCKS):
                    if b % 2 == 0:
                        act.wait_ge(hid_in_ps, 2 * t + b // 2 + 1)
                    psum = hid_ps[s][b // 2][:, b % 2 * SLOT_TILE:(b % 2 + 1) * SLOT_TILE]
                    bias = b1[:, bass.ds(e, 1), b:b + 1]
                    act.activation(hid_hi[:, s, b, :], psum, ACT.Gelu_apprx_tanh, bias=bias, scale=1.0 / WSCALE).then_inc(hid_hi_ok, 1)
                    act.activation(hid[:, s, b, :], psum, ACT.Gelu_apprx_tanh, bias=bias, scale=1.0 / WSCALE).then_inc(hid_ok, 1)

            act.wait_ge(table_ok, 1)
            gelu(0, 0, True)
            gelu(1, 1, True)
            with act.Fori(1, N_TILES // 2) as k:
                gelu(2 * k, 0)
                gelu(2 * k + 1, 1)
            gelu(N_TILES - 1, 0)

        @block.tensor
        def _(pe):
            pe.wait_ge(ld_w, 16)
            pe.wait_ge(dve_set, 1)
            ps = once
            pe.matmul(ps[:, 0:P], wp[:, WQ:WQ + P], wp[:, WK:WK + P], start=True, stop=True)
            pe.matmul(ps[:, P:2 * P], wp[:, WV:WV + P], wp[:, WOT:WOT + P], start=True, stop=True)
            pe.matmul(ps[:, 2 * P:2 * P + 1], wp[:, WK:WK + P], wp[:, BQ:BQ + 1], start=True, stop=True)
            pe.matmul(ps[:, 2 * P + 1:3 * P + 1], out_bias[:], wp[:, WOT:WOT + P], start=True, stop=True).then_inc(fused_ps, 1)

            def values(h):
                if h == 0:
                    pe.wait_ge(ld_ctx, 16)
                for j in range(HALF):
                    t = h * HALF + j
                    mm = pe.matmul(v_bank[h][:, j * P:(j + 1) * P], ctx_sb[:, t * P:(t + 1) * P], fused[:, P:2 * P],
                                   start=True, stop=True)
                mm.then_inc(v_ps, 1)

            def norm_t(h):
                pe.wait_ge(xn_ok, (h + 1) * HALF)
                for j in range(HALF):
                    mm = pe.transpose(xnt_bank[h][:, j * P:(j + 1) * P], xn[:, h * HALF + j, :], ident[:])
                mm.then_inc(xnt_ps, 1)

            def queries(h):
                pe.wait_ge(xnt_ok, h + 1)
                pe.matmul(q_bank[h][:, :], fused[:, 0:P], xn_t[:, h * HALF * P:(h + 1) * HALF * P], start=True, stop=True).then_inc(q_ps, 1)

            def scores(g):
                if g < 2:
                    pe.wait_ge(q_ok, g + 1)
                else:
                    pe.wait_ge(var2_ok, g - 1)
                for j in range(GROUP):
                    for h in range(2):
                        at = (g * GROUP + j) * P + h * SEQ
                        mm = pe.matmul(score[g % 2][h * SEQ:(h + 1) * SEQ, j * SEQ:(j + 1) * SEQ],
                                       q_t[:, at:at + SEQ], ctx_sb[:, at:at + SEQ],
                                       start=True, stop=True)
                mm.then_inc(s_ps, 1)

            def probs_t(g):
                pe.wait_ge(prob_ok, 2 * (g + 1))
                if g >= 2:
                    pe.wait_ge(pt_ok, g - 1)
                for j in range(GROUP):
                    mm = pe.transpose(probs_bank[g % 2][:, j * P:(j + 1) * P], probs[:, g * GROUP + j, :], ident[:])
                mm.then_inc(pt_ps, 1)

            def attend(g):
                pe.wait_ge(pt_ok, g + 1)
                if g == 0:
                    pe.wait_ge(v_ok, 2)
                for j in range(GROUP):
                    pe.matmul(score[g % 2][:, DEN + j:DEN + j + 1], p_t[:, g, j * P:(j + 1) * P], ones_col[:],
                              start=True, stop=True)
                for j in range(GROUP):
                    mm = pe.matmul(score[g % 2][:, j * P:(j + 1) * P], p_t[:, g, j * P:(j + 1) * P],
                                   v_sb[:, (g * GROUP + j) * P:(g * GROUP + j + 1) * P], start=True, stop=True)
                mm.then_inc(o_ps, 1)

            def norm2_t(g):
                pe.wait_ge(xn2_ok, g + 1)
                if g >= 2:
                    pe.wait_ge(group_done, g - 1)
                for j in range(GROUP):
                    mm = pe.transpose(turn[g % 2][:, j * P:(j + 1) * P], xn2[:, g * GROUP + j, :], ident[:])
                mm.then_inc(x2t_ps, 1)

            def route(g):
                pe.wait_ge(x2t_ok, g + 1)
                for j in range(GROUP):
                    at = LOGIT + j * EXPERTS
                    mm = pe.matmul(turn[g % 2][:, at:at + EXPERTS], xn2_t[:, g, j * P:(j + 1) * P],
                                   wp[:, GATEW:GATEW + EXPERTS], start=True, stop=True)
                mm.then_inc(logit_ps, 1)

            def ranks(g):
                pe.wait_ge(chosen_ok, g + 1)
                for j in range(GROUP):
                    t = g * GROUP + j
                    at = RANK + j * EXPERTS
                    mm = pe.matmul(turn[g % 2][:, at:at + EXPERTS], before[:], chosen[:, t, :], start=True, stop=t == 0)
                    for u in range(t):
                        mm = pe.matmul(turn[g % 2][:, at:at + EXPERTS], ones[:], chosen[:, u, :], start=False, stop=u == t - 1)
                mm.then_inc(rank_ps, 1)

            pe.wait_ge(consts, 1)
            pe.wait_ge(fused_ok, 1)
            for h in range(2):
                norm_t(h)
                queries(h)
                values(h)
            for step in range(STEPS):
                for g in range(GROUPS):
                    stage = step - SKEW * g
                    if stage == SCORES:
                        scores(g)
                    elif stage == PROBS_T:
                        probs_t(g)
                    elif stage == ATTEND:
                        attend(g)
                    elif stage == NORM2_T:
                        norm2_t(g)
                    elif stage == ROUTE:
                        route(g)
                    elif stage == RANKS:
                        ranks(g)
            for t in range(TILES):
                mm = pe.matmul(once[:, COUNT:COUNT + EXPERTS], ones[:], chosen[:, t, :],
                               start=t == 0, stop=t == TILES - 1)
            mm.then_inc(count_ps, 1)

            def expert_of(t):
                return pe.value_load(tile_experts[0:1, bass.ds(t, 1)], min_val=0, max_val=EXPERTS - 1)

            def turn_rows(t, s, n):
                pe.wait_ge(loaded[s], 16 * n)
                to = xs_ps[s][:, :].bitcast(F16)
                for r in range(HALVES):
                    pe.transpose(to[:, r * P:(r + 1) * P], in_parts[:, s, r, 0:P], ident16[:])
                for r in range(HALVES):
                    mm = pe.transpose(to[:, SLOT_TILE + r * P:SLOT_TILE + (r + 1) * P], in_parts[:, s, r, P:2 * P], ident16[:])
                mm.then_inc(xs_in_ps, 1)

            def may_hidden(t, first=False):
                pe.wait_ge(xs_ok, t + 1)
                if not first:
                    pe.wait_ge(hid_ok, BLOCKS * (t - 1))

            def hidden(e, s):
                hi, lo = xs_t[:, s, 0, :], xs_t[:, s, 1, :]
                for b in range(BLOCKS):
                    to = hid_ps[s][b // 2][:, b % 2 * SLOT_TILE:(b % 2 + 1) * SLOT_TILE]
                    pe.matmul(to, w1_hi[:, bass.ds(e, 1), b * P:(b + 1) * P], hi, start=True, stop=False)
                    pe.matmul(to, w1_hi[:, bass.ds(e, 1), b * P:(b + 1) * P], lo, start=False, stop=False)
                    mm = pe.matmul(to, w1_lo[:, bass.ds(e, 1), b * P:(b + 1) * P], hi, start=False, stop=True)
                    if b % 2:
                        mm.then_inc(hid_in_ps, 1)

            def output(t, s, e, first=False):
                pe.wait_ge(hid_hi_ok, BLOCKS * (t + 1))
                if not first:
                    pe.wait_ge(y_ok, t)
                for r in range(HALVES):
                    pe.matmul(y_ps[r][:, 0:P], out_sel[:], b2_16[:, bass.ds(e, 1), :], start=True, stop=False)
                for b in range(BLOCKS):
                    for r in range(HALVES):
                        pe.matmul(y_ps[r][:, 0:P], hid_hi[:, s, b, r * P:(r + 1) * P], w2_lo[:, bass.ds(e, 1), b * P:(b + 1) * P],
                                  start=False, stop=False)
                pe.wait_ge(hid_lo_ok, t + 1)
                for b in range(BLOCKS):
                    for r in range(HALVES):
                        pe.matmul(y_ps[r][:, 0:P], hid_hi[:, s, b, r * P:(r + 1) * P], w2_hi[:, bass.ds(e, 1), b * P:(b + 1) * P],
                                  start=False, stop=False)
                        mm = pe.matmul(y_ps[r][:, 0:P], hid_lo[:, s, b, r * P:(r + 1) * P], w2_hi[:, bass.ds(e, 1), b * P:(b + 1) * P],
                                       start=False, stop=b == BLOCKS - 1)
                mm.then_inc(y_in_ps, 1)

            pe.wait_ge(row_ok, GROUPS)
            pe.wait_ge(table_ok, 1)
            pe.wait_ge(w1_ok, GROUPS)
            pe.wait_ge(w2_ok, GROUPS)
            pe.wait_ge(b2_ok, 1)

            def step(t, s, n, e, e_before, first=False):
                may_hidden(t, first)
                turn_rows(t + 1, 1 - s, n)
                hidden(e, s)
                output(t - 1, 1 - s, e_before, first)

            turn_rows(0, 0, 1)
            e = expert_of(0)
            may_hidden(0, True)
            turn_rows(1, 1, 1)
            hidden(e, 0)
            step(1, 1, 2, expert_of(1), e, True)
            step(2, 0, 2, expert_of(2), expert_of(1))
            with pe.Fori(1, N_TILES // 2 - 1) as k:
                e = expert_of(2 * k + 1)
                step(2 * k + 1, 1, k + 2, e, expert_of(2 * k))
                step(2 * k + 2, 0, k + 2, expert_of(2 * k + 2), e)
            last = N_TILES - 1
            e = expert_of(last - 1)
            step(last - 1, 1, last // 2 + 1, e, expert_of(last - 2))
            may_hidden(last)
            e_last = expert_of(last)
            hidden(e_last, 0)
            output(last - 1, 1, e)
            output(last, 0, e_last)

        @block.vector
        def _(v):
            done = 0

            def then(instruction):
                nonlocal done
                instruction.then_inc(dve, 1)
                done += 1
                return done

            v.memset(b2_in[:], 0.0).then_inc(zeroed, 1)
            v.memset(ones[:], 1.0)
            then(v.memset(b2_16[:], 0.0))
            v.wait_ge(ld_w, 16)
            v.tensor_copy(out_bias[:], wp[:, BV:BV + 1].to_broadcast((P, P))).then_inc(dve_set, 1)

            for i in range(2):
                tiles = range(i * HALF, (i + 1) * HALF)
                v.wait_ge(ld_x[i], 16)
                for t in tiles:
                    n = then(v.bn_stats(stats[:, t, :], x_sb[:, t, :]))
                v.wait_ge(dve, n)
                for t in tiles:
                    n = then(v.bn_aggr(meanvar[:, t, :], stats[:, t, :]))
                v.wait_ge(dve, n)
                h = slice(i * HALF, (i + 1) * HALF)
                v.tensor_scalar(var_eps[:, h], meanvar[:, h, 1], EPS, None, ALU.add).then_inc(var_ok, 1)
            for t in range(TILES):
                v.wait_ge(rstd_ok, t // HALF + 1)
                v.tensor_scalar(xn[:, t, :], x_sb[:, t, :], meanvar[:, t, 0:1], rstd[:, t:t + 1],
                                ALU.subtract, ALU.mult).then_inc(xn_ok, 1)
            v.wait_ge(fused_ok, 1)
            n = then(v.tensor_tensor(out_bias[:], fused[:, 2 * P + 1:3 * P + 1], wp[:, BO:BO + P], ALU.add))
            v.wait_ge(dve, n)
            v.wait_ge(tanh_ok, 1)
            v.tensor_scalar(out_bias[:], out_bias[:], tanhs[:, 0:1], None, ALU.mult).then_inc(bias_ok, 1)
            v.wait_ge(consts, 1)
            then(v.tensor_copy(iota_e[:], iota_i[:]))
            then(v.tensor_copy(region[:], region_i[:]))
            then(v.tensor_copy(tile_no[:], tile_i[:]))
            then(v.tensor_copy(edge[:], edge_i[:]))
            then(v.tensor_copy(run_from[:], run_i[:]))
            made = then(v.tensor_copy(rows[:, :, :, TARGET], target[:]))

            def score_max(g):
                s = score[g % 2][:, 0:GROUP * SEQ].rearrange("p (j s) -> p j s", j=GROUP)
                v.wait_ge(s_ps, g + 1)
                n = then(v.tensor_reduce(s_max[:, g, :], s, AX_X, ALU.max))
                v.wait_ge(dve, n)
                v.tensor_tensor(s_sub[:, g, :, :], s, s_max[:, g, :, None].to_broadcast((P, GROUP, SEQ)),
                                ALU.subtract).then_inc(sub_ok, 1)

            def residual(g):
                v.wait_ge(o_ps, g + 1)
                n = then(v.reciprocal(rden[:, g, :], score[g % 2][:, DEN:DEN + GROUP]))
                v.wait_ge(dve, n)
                n = then(v.tensor_scalar(rgate[:, g, :], rden[:, g, :], tanhs[:, 0:1], None, ALU.mult))
                v.wait_ge(dve, n)
                v.wait_ge(xbias_ok, 1)
                for j in range(GROUP):
                    t = g * GROUP + j
                    n = then(v.scalar_tensor_tensor(x1[:, t, :], score[g % 2][:, j * P:(j + 1) * P], rgate[:, g, j:j + 1],
                                                    x_bias[:, t, :], ALU.mult, ALU.add))
                v.wait_ge(dve, n)
                for t in range(g * GROUP, (g + 1) * GROUP):
                    n = then(v.bn_stats(stats2[:, t, :], x1[:, t, :]))
                v.wait_ge(dve, n)
                for t in range(g * GROUP, (g + 1) * GROUP):
                    n = then(v.bn_aggr(meanvar2[:, t, :], stats2[:, t, :]))
                v.wait_ge(dve, n)
                v.tensor_scalar(var_eps2[:, group(g)], meanvar2[:, group(g), 1], EPS, None, ALU.add).then_inc(var2_ok, 1)

            def norm2(g):
                v.wait_ge(rstd2_ok, g + 1)
                for t in range(g * GROUP, (g + 1) * GROUP):
                    m = v.tensor_scalar(xn2[:, t, :], x1[:, t, :], meanvar2[:, t, 0:1], rstd2[:, t:t + 1],
                                        ALU.subtract, ALU.mult)
                m.then_inc(xn2_ok, 1)

            def choose(g):
                v.wait_ge(logit_ps, g + 1)
                n = then(v.tensor_copy(logits[:, group(g), :], turn[g % 2][:, LOGIT:LOGIT + GROUP * EXPERTS].rearrange(
                    "p (j e) -> p j e", j=GROUP)))
                v.wait_ge(dve, n)
                for t in range(g * GROUP, (g + 1) * GROUP):
                    n = then(v.max(sorted_l[:, t, :], logits[:, t, :]))
                v.wait_ge(dve, n)
                for t in range(g * GROUP, (g + 1) * GROUP):
                    n = then(v.max_index(index[:, t, :], sorted_l[:, t, :], logits[:, t, :]))
                v.tensor_tensor(shifted[:, group(g), :], sorted_l[:, group(g), :],
                                sorted_l[:, group(g), 0:1].to_broadcast((P, GROUP, EXPERTS)), ALU.subtract).then_inc(shift_ok, 1)
                v.wait_ge(dve, n)
                n = then(v.tensor_copy(index_f[:, group(g), :], index[:, group(g), 0:TOP_K]))
                v.wait_ge(dve, n)
                n = then(v.tensor_tensor(choice[:, group(g), :, :], iota_e[:, None, None, :].to_broadcast((P, GROUP, TOP_K, EXPERTS)),
                                         index_f[:, group(g), :, None].to_broadcast((P, GROUP, TOP_K, EXPERTS)), ALU.is_equal))
                v.wait_ge(dve, n)
                v.tensor_tensor(chosen[:, group(g), :], choice[:, group(g), 0, :], choice[:, group(g), 1, :],
                                ALU.add).then_inc(chosen_ok, 1)

            def fill_rows_of(g):
                for k in range(TOP_K):
                    v.wait_ge(hi_ok, TOP_K * g + k + 1)
                    then(v.tensor_tensor(row_parts[:, group(g), k, P:2 * P], xn2[:, group(g), :], row_parts[:, group(g), k, 0:P], ALU.subtract))
                v.wait_ge(exps_ok, g + 1)
                n = then(v.tensor_reduce(exp_sum[:, group(g)], exps[:, group(g), :], AX_X, ALU.add))
                v.wait_ge(dve, n)
                n = then(v.reciprocal(exp_rec[:, group(g)], exp_sum[:, group(g)]))
                v.wait_ge(dve, n)
                n = then(v.tensor_tensor(gates[:, group(g), :], exps[:, group(g), 0:TOP_K],
                                         exp_rec[:, group(g), None].to_broadcast((P, GROUP, TOP_K)), ALU.mult))
                v.wait_ge(dve, n)
                then(v.tensor_scalar(rows[:].bitcast(F32)[:, group(g), :, GATE], gates[:, group(g), :], tanhs[:, 1:2],
                                     1.0 / WSCALE, ALU.mult, ALU.mult))
                v.wait_ge(rank_ps, g + 1)
                v.tensor_tensor(place[:, group(g), :], turn[g % 2][:, RANK:RANK + GROUP * EXPERTS].rearrange("p (j e) -> p j e", j=GROUP),
                                region[:, None, :].to_broadcast((P, GROUP, EXPERTS)), ALU.add).then_inc(group_done, 1)
                v.wait_ge(group_done, g + 1)
                n = then(v.tensor_tensor(place_k[:, group(g), :, :], choice[:, group(g), :, :],
                                         place[:, group(g), None, :].to_broadcast((P, GROUP, TOP_K, EXPERTS)), ALU.mult))
                v.wait_ge(dve, n)
                n = then(v.tensor_reduce(slot_f[:, group(g), :], place_k[:, group(g), :, :], AX_X, ALU.add))
                v.wait_ge(dve, n)
                v.tensor_copy(slot[:, TOP_K * g * GROUP:TOP_K * (g + 1) * GROUP],
                              slot_f[:, group(g), :].rearrange("p t k -> p (t k)")).then_inc(row_ok, 1)

            def weights_lo(to, at, hi, hi_made, made_lo, i):
                q = experts_of(i)
                v.wait_ge(hi_made, i + 1)
                v.scalar_tensor_tensor(to[:, q, :], at[:, q, :], WSCALE, hi[:, q, :], ALU.mult, ALU.subtract).then_inc(made_lo, 1)

            v.wait_ge(ld_b, 32)
            n = then(v.tensor_scalar(b2_hi[:], b2_in[:], WSCALE, None, ALU.mult))
            v.wait_ge(dve, n)
            parts = b2_16[:].rearrange("p e f -> p (e f)")
            v.scalar_tensor_tensor(parts[32:33, :], b2_in[32:33, :], WSCALE, b2_hi[32:33, :], ALU.mult, ALU.subtract)
            v.tensor_copy(parts[0:1, :], b2_hi[0:1, :]).then_inc(b2_ok, 1)
            v.wait_ge(dve, made)
            for step in range(STEPS):
                for g in range(GROUPS):
                    stage = step - SKEW * g
                    if stage == MAXIMUM:
                        score_max(g)
                    elif stage == RESIDUAL:
                        residual(g)
                    elif stage == NORM2:
                        norm2(g)
                        weights_lo(w1_lo, w1_sb, w1_hi, w1hi_ok, w1_ok, g)
                    elif stage == CHOOSE:
                        choose(g)
                    elif stage == FILL:
                        fill_rows_of(g)
                        if g < GROUPS - 1:
                            weights_lo(w2_lo, w2_sb, w2_hi, w2hi_ok, w2_ok, g)

            v.wait_ge(count_ps, 1)
            then(v.tensor_copy(counts[:], once[0:1, COUNT:COUNT + EXPERTS]))
            n = then(v.tensor_tensor(run_row[:], once[:, COUNT:COUNT + EXPERTS], run_from[:], ALU.add))
            v.wait_ge(dve, n)
            then(v.tensor_tensor(run_word[:], run_row[:], run_sel[:], ALU.mult))
            n = then(v.tensor_tensor(over[:], counts[:, :, None].to_broadcast((1, EXPERTS, EDGES)), edge[:], ALU.is_gt))
            v.wait_ge(dve, n)
            then(v.tensor_reduce(pad_at[:], run_word[:], AX_X, ALU.add))
            n = then(v.tensor_reduce(n_tiles[:], over[:], AX_X, ALU.add))
            v.wait_ge(dve, n)
            v.tensor_copy(pad_slot[:], pad_at[:]).then_inc(pads_ok, 1)
            n = then(v.tensor_tensor(upto_n[:], upto[:], n_tiles[:, None, :].to_broadcast((1, EXPERTS, EXPERTS)), ALU.mult))
            v.wait_ge(dve, n)
            n = then(v.tensor_reduce(ends[:], upto_n[:], AX_X, ALU.add))
            v.wait_ge(dve, n)
            n = then(v.tensor_tensor(past[:], tile_no[:], ends[:, None, :].to_broadcast((1, N_TILES, EXPERTS)), ALU.is_ge))
            v.wait_ge(dve, n)
            then(v.tensor_reduce(tile_e[:], past[:], AX_X, ALU.add))
            n = then(v.tensor_tensor(past_n[:], past[:], n_tiles[:, None, :].to_broadcast((1, N_TILES, EXPERTS)), ALU.mult))
            v.wait_ge(dve, n)
            n = then(v.tensor_reduce(tile_base[:], past_n[:], AX_X, ALU.add))
            v.wait_ge(dve, n)
            then(v.tensor_scalar(tile_experts[:], tile_e[:], float(EXPERTS - 1), None, ALU.min))
            n = then(v.tensor_tensor(tile_row[:], tile_no[:, :, 0], tile_base[:], ALU.subtract))
            v.wait_ge(dve, n)
            n = then(v.tensor_scalar(tile_row2[:], tile_e[:], float(REGION // SLOT_TILE), None, ALU.mult))
            v.wait_ge(dve, n)
            n = then(v.tensor_tensor(tile_base[:], tile_row[:], tile_row2[:], ALU.add))
            v.wait_ge(dve, n)
            v.tensor_scalar(tile_rows[:], tile_base[:], float(SLOT_TILE), float(PAD_ROW), ALU.mult, ALU.min).then_inc(table_ok, 1)

            weights_lo(w2_lo, w2_sb, w2_hi, w2hi_ok, w2_ok, GROUPS - 1)

            def copy_rows(t, s, first=False):
                v.wait_ge(xs_in_ps, t + 1)
                if not first:
                    v.wait_ge(hid_in_ps, t - 1)
                v.tensor_copy(xs_t[:, s, :, :], xs_ps[s][:, :].bitcast(F16)[:, 0:2 * SLOT_TILE].rearrange("p (c s) -> p c s", c=2)).then_inc(xs_ok, 1)
                if not first:
                    v.wait_ge(aim_ok, t - 1)
                v.tensor_copy(ahead[:, s, :, :], in_rows[:, s, :, TARGET:GATE + 1]).then_inc(row_read, 1)

            def low_part(t, s, first=False):
                v.wait_ge(hid_ok, BLOCKS * (t + 1))
                if not first:
                    v.wait_ge(y_in_ps, t - 1)
                v.tensor_tensor(hid_lo[:, s, :, :], hid[:, s, :, :], hid_hi[:, s, :, :], ALU.subtract).then_inc(hid_lo_ok, 1)

            def keep_aims(t, s, sent_before):
                v.wait_ge(row_read, t + 1)
                if sent_before is not None:
                    v.wait_ge(scattered[s], 16 * HALVES * sent_before)
                v.tensor_copy(aims[:, s, :, :], ahead[:, s, :, :]).then_inc(aim_ok, 1)

            def gated(t, s):
                v.wait_ge(y_in_ps, t + 1)
                v.wait_ge(aim_ok, t + 1)
                for r in range(HALVES):
                    m = v.tensor_scalar(y_sb[:, s, r, :], y_ps[r][:, 0:P], aims[:].bitcast(F32)[:, s, r, 1:2], None, ALU.mult)
                m.then_inc(y_ok, 1)

            copy_rows(0, 0, True)
            copy_rows(1, 1, True)
            keep_aims(0, 0, None)
            copy_rows(2, 0)
            low_part(0, 0, True)
            gated(0, 0)
            keep_aims(1, 1, None)
            copy_rows(3, 1)
            low_part(1, 1, True)
            gated(1, 1)
            with v.Fori(1, N_TILES // 2 - 1) as k:
                keep_aims(2 * k, 0, k)
                copy_rows(2 * k + 2, 0)
                low_part(2 * k, 0)
                gated(2 * k, 0)
                keep_aims(2 * k + 1, 1, k)
                copy_rows(2 * k + 3, 1)
                low_part(2 * k + 1, 1)
                gated(2 * k + 1, 1)
            last = N_TILES - 1
            keep_aims(last - 2, 0, last // 2 - 1)
            copy_rows(last, 0)
            low_part(last - 2, 0)
            gated(last - 2, 0)
            keep_aims(last - 1, 1, last // 2 - 1)
            low_part(last - 1, 1)
            gated(last - 1, 1)
            keep_aims(last, 0, last // 2)
            low_part(last, 0)
            gated(last, 0)

            for i in range(4):
                q = slice(2 * i, 2 * i + 2)
                v.wait_ge(ld_res[i], 32)
                n = then(v.tensor_tensor(out_sb[:, q, :], x1[:, q, :], res[:, 0, q, :], ALU.add))
                v.wait_ge(dve, n)
                v.tensor_tensor(out_sb[:, q, :], out_sb[:, q, :], res[:, 1, q, :], ALU.add).then_inc(out_ok, 1)


def kernel(**inputs):
    import numpy as np
    import concourse.bacc as bacc
    from concourse.bass_utils import run_bass_kernel_spmd

    a = {name: np.asarray(value) for name, value in inputs.items()}
    wide = [a["L0_xattn_Wq"], a["L0_xattn_Wk"], a["L0_xattn_Wv"], a["L0_xattn_Wo"].T, a["L0_ffn_gate_w"].T,
            a["L0_xattn_bq"][:, None], a["L0_xattn_bv"][:, None],
            np.broadcast_to(a["L0_xattn_bo"][None, :], (P, P)),
            np.broadcast_to(a["g_xattn"][None, :], (P, 1)), np.broadcast_to(a["g_ffn"][None, :], (P, 1)),
            a["L0_ffn_b1"].reshape(EXPERTS * BLOCKS, P).T]
    arrays = {
        "x": a["x"].reshape(TOKENS, P),
        "ctx_t": a["ctx_1024"].reshape(TOKENS, P).T,
        "wpack": np.concatenate(wide, axis=1),
        "b2": a["L0_ffn_b2"].reshape(1, EXPERTS * P),
        "w1": a["L0_ffn_w1"].transpose(2, 1, 0),
        "w2": a["L0_ffn_w2"].reshape(P, EXPERTS, BLOCKS, P).transpose(3, 1, 2, 0).reshape(P, EXPERTS, FF),
    }
    arrays = {f"in_{name}": np.ascontiguousarray(value) for name, value in arrays.items()}

    nc = bacc.Bacc("TRN2", target_bir_lowering=False, num_devices=1)
    args = [nc.dram_tensor(name, value.shape, mybir.dt.from_np(value.dtype), kind="ExternalInput").ap()
            for name, value in arrays.items()]
    out = nc.dram_tensor("out", (TOKENS, P), F32, kind="ExternalOutput").ap()
    gated_block(nc, *args, out)
    result = run_bass_kernel_spmd(nc, [arrays], core_ids=[0])
    return result.results[0]["out"].reshape(BATCH, SEQ, P)
```

```python
from contextlib import ExitStack

import concourse.bass as bass
from concourse import mybir

ALU = mybir.AluOpType
ACT = mybir.ActivationFunctionType
AX_X = mybir.AxisListType.X
F32, F16, BF16 = mybir.dt.float32, mybir.dt.float16, mybir.dt.bfloat16
I32, U32 = mybir.dt.int32, mybir.dt.uint32

P = 128
BATCH, SEQ = 16, 64
TOKENS = BATCH * SEQ
TILES = TOKENS // P
GROUP = 2
GROUPS = TILES // GROUP
EXPERTS, TOP_K, FF = 8, 2, 512
BLOCKS = FF // P
SLOTS = TOP_K * TOKENS
HALVES = 2
SLOT_TILE = HALVES * P
EDGES = TOKENS // SLOT_TILE
REGION = TOKENS + SLOT_TILE
RUNS = P // EXPERTS
PAD_RUN = SLOT_TILE // RUNS
PAD_ROW = EXPERTS * REGION
N_TILES = (SLOTS - EXPERTS) // SLOT_TILE + EXPERTS
AHEAD = 12
ROW = P + 2
TARGET, GATE = P, P + 1
NO_TARGET = 4 * SLOTS
EPS = 1e-5
WSCALE = 16.0
SCORE_SCALE = float(P) ** -0.5
(NORM_T, COPY_NORM_T, QUERIES, COPY_QUERIES, SCORES, MAXIMUM, EXPONENT, PROBS_T, COPY_PROBS_T, ATTEND, RESIDUAL,
 CENTRED_T, COPY_CENTRED_T, ROUTE, CHOOSE, RANKS, FILL, SEND) = range(18)
SKEW = 4
STEPS = SKEW * (GROUPS - 1) + SEND + 1
W1_STEPS, W2_STEPS, W2_LO_STEPS = [1, 3, 6, 7], [9, 11, 13, 15], []
WQ, WK, WV, WOT, GATEW, BQ, BV, BO, GX, GF, B1 = 0, P, 2 * P, 3 * P, 4 * P, 4 * P + 8, 4 * P + 9, 4 * P + 10, 5 * P + 10, 5 * P + 11, 5 * P + 12
WCOLS = B1 + EXPERTS * BLOCKS


def gated_block(nc, x, ctx_t, wpack, b2, w1, w2, out):
    ctx = ExitStack()
    with ctx:
        def sb(name, shape, dt):
            return ctx.enter_context(nc.sbuf_tensor(name, shape, dt))

        def sem(name):
            return ctx.enter_context(nc.semaphore(name))

        rows_dram = nc.dram_tensor("dispatched", [PAD_ROW + SLOT_TILE, ROW], I32, kind="Internal").ap()
        results_dram = nc.dram_tensor("results", [SLOTS, P], F32, kind="Internal").ap()

        ident = sb("ident", [P, P], F32)
        ident16 = sb("ident16", [P, P], F16)
        before = sb("before", [P, P], BF16)
        ones = sb("ones", [P, P], BF16)
        iota_i = sb("iota_i", [P, EXPERTS], I32)
        region_i = sb("region_i", [P, EXPERTS], I32)
        region = sb("region", [P, EXPERTS], F32)
        target = sb("target", [P, TILES, TOP_K], I32)
        pad_rows = sb("pad_rows", [P, PAD_RUN, ROW], I32)
        run_sel = sb("run_sel", [P, EXPERTS], F32)
        run_i = sb("run_i", [P, EXPERTS], I32)
        run_from = sb("run_from", [P, EXPERTS], F32)
        run_row = sb("run_row", [P, EXPERTS], F32)
        run_word = sb("run_word", [P, EXPERTS], F32)
        pad_at = sb("pad_at", [P, 1], F32)
        pad_slot = sb("pad_slot", [P, 1], U32)
        minus_half = sb("minus_half", [P, TILES], F32)
        out_sel = sb("out_sel", [33, P], F16)
        tile_i = sb("tile_i", [1, N_TILES, EXPERTS], I32)
        tile_no = sb("tile_no", [1, N_TILES, EXPERTS], F32)
        edge_i = sb("edge_i", [1, EXPERTS, EDGES], I32)
        edge = sb("edge", [1, EXPERTS, EDGES], F32)
        upto = sb("upto", [1, EXPERTS, EXPERTS], F32)

        x_sb = sb("x_sb", [P, TILES, P], F32)
        ctx_sb = sb("ctx_sb", [P, TOKENS], F32)
        wp = sb("wp", [P, WCOLS], F32)
        b2_in = sb("b2_in", [33, EXPERTS * P], F32)
        w1_sb = sb("w1_sb", [P, EXPERTS, FF], F32)
        w2_sb = sb("w2_sb", [P, EXPERTS, FF], F32)

        w1_hi = sb("w1_hi", [P, EXPERTS, FF], F16)
        w1_lo = sb("w1_lo", [P, EXPERTS, FF], F16)
        w2_hi = sb("w2_hi", [P, EXPERTS, FF], F16)
        w2_lo = sb("w2_lo", [P, EXPERTS, FF], F16)
        b2_hi = sb("b2_hi", [33, EXPERTS * P], F16)
        b2_16 = sb("b2_16", [33, EXPERTS, P], F16)

        fused = sb("fused", [P, 3 * P + 1], F32)
        tanhs = sb("tanhs", [P, 2], F32)
        out_bias = sb("out_bias", [P, P], F32)
        x_bias = sb("x_bias", [P, TILES, P], F32)
        stats = sb("stats", [P, TILES, 6], F32)
        meanvar = sb("meanvar", [P, TILES, 2], F32)
        var_eps = sb("var_eps", [P, TILES], F32)
        rstd = sb("rstd", [P, TILES], F32)
        xn = sb("xn", [P, TILES, P], F32)
        xn_t = sb("xn_t", [P, TOKENS], F32)
        q_t = sb("q_t", [P, TOKENS], F32)
        v_sb = sb("v_sb", [P, TILES, P + 1], F32)
        s_max = sb("s_max", [P, GROUPS, GROUP], F32)
        s_sub = sb("s_sub", [P, GROUPS, GROUP, SEQ], F32)
        probs = sb("probs", [P, TILES, P], F32)
        p_t = sb("p_t", [P, GROUPS, GROUP * P], F32)
        rden = sb("rden", [P, GROUPS, GROUP], F32)
        x1 = sb("x1", [P, TILES, P], F32)

        stats2 = sb("stats2", [P, TILES, 6], F32)
        meanvar2 = sb("meanvar2", [P, TILES, 2], F32)
        var_eps2 = sb("var_eps2", [P, TILES], F32)
        rstd2 = sb("rstd2", [P, TILES], F32)
        centred = sb("centred", [P, TILES, P], F32)
        centred_t = sb("centred_t", [P, GROUPS, GROUP * P], F32)
        logits = sb("logits", [P, TILES, EXPERTS], F32)
        sorted_l = sb("sorted_l", [P, TILES, EXPERTS], F32)
        index = sb("index", [P, TILES, EXPERTS], U32)
        choice = sb("choice", [P, TILES, TOP_K, EXPERTS], F32)
        chosen = sb("chosen", [P, TILES, EXPERTS], BF16)
        shifted = sb("shifted", [P, TILES, EXPERTS], F32)
        exps = sb("exps", [P, TILES, EXPERTS], F32)
        exp_sum = sb("exp_sum", [P, TILES], F32)
        exp_rec = sb("exp_rec", [P, TILES], F32)
        gate_scale = sb("gate_scale", [P, 1], F32)
        place = sb("place", [P, TILES, EXPERTS], F32)
        place_k = sb("place_k", [P, TILES, TOP_K, EXPERTS], F32)
        slot_f = sb("slot_f", [P, TILES, TOP_K], F32)
        slot = sb("slot", [P, TOP_K * TILES], U32)
        rows = sb("rows", [P, TILES, TOP_K, ROW], I32)

        counts = sb("counts", [1, EXPERTS], F32)
        over = sb("over", [1, EXPERTS, EDGES], F32)
        n_tiles = sb("n_tiles", [1, EXPERTS], F32)
        upto_n = sb("upto_n", [1, EXPERTS, EXPERTS], F32)
        ends = sb("ends", [1, EXPERTS], F32)
        past = sb("past", [1, N_TILES, EXPERTS], F32)
        past_n = sb("past_n", [1, N_TILES, EXPERTS], F32)
        tile_e = sb("tile_e", [1, N_TILES], F32)
        tile_base = sb("tile_base", [1, N_TILES], F32)
        tile_row = sb("tile_row", [1, N_TILES], F32)
        tile_row2 = sb("tile_row2", [1, N_TILES], F32)
        tile_rows = sb("tile_rows", [1, N_TILES], I32)
        tile_experts = sb("tile_experts", [1, N_TILES], I32)

        in_rows = sb("in_rows", [P, 2, HALVES, ROW], I32)
        xs_t = sb("xs_t", [P, 2, 2, SLOT_TILE], F16)
        hid = sb("hid", [P, 2, BLOCKS, SLOT_TILE], F32)
        hid_hi = sb("hid_hi", [P, 2, BLOCKS, SLOT_TILE], F16)
        hid_lo = sb("hid_lo", [P, 2, BLOCKS, SLOT_TILE], F16)
        y_sb = sb("y_sb", [P, N_TILES, HALVES, P], F32)
        aims = sb("aims", [P, N_TILES, HALVES, 2], I32)

        row_parts, in_parts = rows[:].bitcast(F16), in_rows[:].bitcast(F16)

        res = sb("res", [P, TILES, TOP_K, P], F32)
        out_sb = sb("out_sb", [P, TILES, P], F32)

        bank = [ctx.enter_context(nc.psum_tensor(f"bank{i}", [P, 512], F32)) for i in range(8)]
        once = bank[0]
        v_bank = [bank[1], bank[5]]
        once = bank[0]
        xnt_bank = bank[4]
        q_bank = bank[7]
        turn = [bank[1], bank[5]]
        probs_bank = [bank[2], bank[6]]
        score = [bank[3], bank[0]]
        LOGIT, RANK, COUNT = 408, 432, 0
        xs_ps = [bank[0], bank[4]]
        hid_ps = [[bank[1], bank[3]], [bank[5], bank[7]]]
        y_ps = [bank[2], bank[6]]

        ld_x, ld_ctx, ld_w = [sem(f"ld_x{i}") for i in range(2)], sem("ld_ctx"), sem("ld_w")
        ld_b, ld_w1, ld_w2 = sem("ld_b"), sem("ld_w1"), sem("ld_w2")
        pool_set, ident_ok, probs_zero, consts = sem("pool_set"), sem("ident_ok"), sem("probs_zero"), sem("consts")
        dve_set, pads_set = sem("dve_set"), sem("pads_set")
        zeroed = sem("zeroed")
        fused_ps, fused_ok, tanh_ok = sem("fused_ps"), sem("fused_ok"), sem("tanh_ok")
        bias_ok, xbias_ok = sem("bias_ok"), sem("xbias_ok")
        dve = sem("dve")
        var_ok, rstd_ok, xn_ok = sem("var_ok"), sem("rstd_ok"), sem("xn_ok")
        v_ps, v_ok, v_ones = sem("v_ps"), sem("v_ok"), sem("v_ones")
        xnt_ps, xnt_ok, q_ps, q_ok = sem("xnt_ps"), sem("xnt_ok"), sem("q_ps"), sem("q_ok")
        s_ps, sub_ok, prob_ok = sem("s_ps"), sem("sub_ok"), sem("prob_ok")
        pt_ps, pt_ok, o_ps = sem("pt_ps"), sem("pt_ok"), sem("o_ps")
        var2_ok, rstd2_ok, centred_ok = sem("var2_ok"), sem("rstd2_ok"), sem("centred_ok")
        ct_ps, ct_ok, logit_ps = sem("ct_ps"), sem("ct_ok"), sem("logit_ps")
        chosen_ok, rank_ps, shift_ok, exps_ok = sem("chosen_ok"), sem("rank_ps"), sem("shift_ok"), sem("exps_ok")
        hi_ok, row_ok = sem("hi_ok"), sem("row_ok")
        group_done = sem("group_done")
        sent = sem("sent")
        padded, pads_ok, filled = sem("padded"), sem("pads_ok"), sem("filled")
        count_ps, table_ok = sem("count_ps"), sem("table_ok")
        w1hi_ok, w1_ok, w2hi_ok, w2_ok, b2_ok = sem("w1hi_ok"), sem("w1_ok"), sem("w2hi_ok"), sem("w2_ok"), sem("b2_ok")
        loaded = [sem(f"loaded{i}") for i in range(2)]
        xs_in_ps, xs_ok, hid_in_ps, hid_hi_ok, hid_ok, hid_lo_ok = sem("xs_in_ps"), sem("xs_ok"), sem("hid_in_ps"), sem("hid_hi_ok"), sem("hid_ok"), sem("hid_lo_ok")
        y_in_ps, y_ok, row_read = sem("y_in_ps"), sem("y_ok"), sem("row_read")
        scattered = sem("scattered")
        ld_res, out_ok, stored = [sem(f"ld_res{i}") for i in range(4)], sem("out_ok"), sem("stored")

        x_view = x.rearrange("(t p) d -> p t d", p=P)
        out_view = out.rearrange("(t p) d -> p t d", p=P)
        res_view = results_dram.rearrange("(t k p) d -> p t k d", p=P, k=TOP_K)
        HALF = TILES // 2

        def experts_of(g):
            return slice(g * EXPERTS // GROUPS, (g + 1) * EXPERTS // GROUPS)

        def group(g):
            return slice(g * GROUP, (g + 1) * GROUP)

        block = ctx.enter_context(nc.Block())

        @block.sync
        def _(sp):
            for i in range(2):
                sp.dma_start(x_sb[:, i * HALF:(i + 1) * HALF, :], x_view[:, i * HALF:(i + 1) * HALF, :]).then_inc(ld_x[i], 16)
            sp.dma_start(ctx_sb[:], ctx_t).then_inc(ld_ctx, 16)
            sp.dma_start(w1_sb[:], w1).then_inc(ld_w1, 16)
            sp.wait_ge(zeroed, 1)
            for i in range(2):
                sp.dma_start(b2_in[32 * i:32 * i + 1, :], b2).then_inc(ld_b, 16)
            sp.dma_start(w2_sb[:], w2).then_inc(ld_w2, 16)
            sp.wait_ge(pads_set, 1)
            sp.dma_start(rows_dram[PAD_ROW:PAD_ROW + SLOT_TILE, :].rearrange("(p r) c -> p r c", r=HALVES), pad_rows[:, 0:HALVES, :]).then_inc(padded, 16)
            sp.wait_ge(table_ok, 1)
            first = [sp.value_load(tile_rows[0:1, t:t + 1], min_val=0, max_val=PAD_ROW) for t in range(2)]
            sp.wait_ge(sent, 16 * SLOTS // P)
            sp.wait_ge(filled, 16)
            sp.wait_ge(padded, 16)

            def load_rows(at, s):
                sp.dma_start(in_rows[:, s, :, :], rows_dram[bass.ds(at, SLOT_TILE), :].rearrange("(p r) c -> p r c", r=HALVES)).then_inc(loaded[s], 16)

            def next_rows(t, s):
                at = sp.value_load(tile_rows[0:1, bass.ds(t, 1)], min_val=0, max_val=PAD_ROW)
                sp.wait_ge(row_read, t - 1)
                load_rows(at, s)

            load_rows(first[0], 0)
            load_rows(first[1], 1)
            with sp.Fori(1, N_TILES // 2) as k:
                next_rows(2 * k, 0)
                next_rows(2 * k + 1, 1)
            next_rows(N_TILES - 1, 0)
            sp.wait_ge(scattered, 16 * HALVES * N_TILES)
            for i in range(4):
                q = slice(2 * i, 2 * i + 2)
                sp.dma_start(res[:, q, :, :], res_view[:, q, :, :]).then_inc(ld_res[i], 16)
            for i in range(4):
                q = slice(2 * i, 2 * i + 2)
                sp.wait_ge(out_ok, i + 1)
                sp.dma_start(out_view[:, q, :], out_sb[:, q, :]).then_inc(stored, 16)
            sp.wait_ge(stored, 64)

        def send(pool, g):
            pool.wait_ge(row_ok, g + 1)
            for t in range(g * GROUP, (g + 1) * GROUP):
                for k in range(TOP_K):
                    j = TOP_K * t + k
                    pool.indirect_dma_start(rows_dram, bass.IndirectOffsetOnAxis(ap=slot[:, j:j + 1], axis=0),
                                            rows[:, t, k, :], None).then_inc(sent, 16)

        @block.gpsimd
        def _(pool):
            pool.memset(ident[:], 0.0).then_inc(pool_set, 1)
            pool.memset(minus_half[:], -0.5).then_inc(pool_set, 1)
            pool.wait_ge(pool_set, 2)
            pool.affine_select(out=ident[:], in_=ident[:], compare_op=ALU.not_equal, fill=1.0, base=0,
                               pattern=[[-1, P]], channel_multiplier=1).then_inc(ident_ok, 1)
            pool.iota(iota_i[:], [[1, EXPERTS]], base=0, channel_multiplier=0).then_inc(pool_set, 1)
            pool.iota(region_i[:], [[REGION, EXPERTS]], base=0, channel_multiplier=0).then_inc(pool_set, 1)
            pool.iota(target[:], [[TOP_K * P, TILES], [P, TOP_K]], base=0, channel_multiplier=1).then_inc(pool_set, 1)
            pool.iota(tile_i[:], [[1, N_TILES], [0, EXPERTS]], base=0, channel_multiplier=0).then_inc(pool_set, 1)
            pool.iota(run_i[:], [[REGION - SLOT_TILE, EXPERTS]], base=0, channel_multiplier=PAD_RUN).then_inc(pool_set, 1)
            pool.iota(edge_i[:], [[0, EXPERTS], [SLOT_TILE, EDGES]], base=0, channel_multiplier=0).then_inc(pool_set, 1)
            for i in range(2):
                h = slice(i * HALF, (i + 1) * HALF)
                pool.wait_ge(var_ok, i + 1)
                pool.tensor_tensor(rstd[:, h], var_eps[:, h], minus_half[:, h], ALU.pow).then_inc(rstd_ok, 1)
            pool.memset(probs[:], 0.0).then_inc(probs_zero, 1)
            for m in (ident16, out_sel):
                pool.memset(m[:], 0.0).then_inc(pool_set, 1)
            pool.memset(before[:], 1.0).then_inc(pool_set, 1)
            pool.memset(upto[:], 1.0).then_inc(pool_set, 1)
            pool.memset(run_sel[:], float(ROW)).then_inc(pool_set, 1)
            pool.wait_ge(pool_set, 13)
            pool.affine_select(out=ident16[:], in_=ident16[:], compare_op=ALU.not_equal, fill=1.0, base=0,
                               pattern=[[-1, P]], channel_multiplier=1).then_inc(pool_set, 1)
            pool.affine_select(out=before[:], in_=before[:], compare_op=ALU.is_gt, fill=0.0, base=0,
                               pattern=[[1, P]], channel_multiplier=-1).then_inc(pool_set, 1)
            pool.affine_select(out=upto[:], in_=upto[:], compare_op=ALU.is_ge, fill=0.0, base=0,
                               pattern=[[1, EXPERTS], [-1, EXPERTS]], channel_multiplier=0).then_inc(pool_set, 1)
            pool.affine_select(out=run_sel[:], in_=run_sel[:], compare_op=ALU.is_ge, fill=0.0, base=0,
                               pattern=[[-RUNS, EXPERTS]], channel_multiplier=1).then_inc(pool_set, 1)
            for i in range(2):
                if i:
                    pool.wait_ge(pool_set, 18)
                pool.affine_select(out=out_sel[:], in_=out_sel[:], compare_op=ALU.not_equal, fill=1.0,
                                   base=-32 * i, pattern=[[0, P]], channel_multiplier=1).then_inc(pool_set, 1)
            pool.affine_select(out=run_sel[:], in_=run_sel[:], compare_op=ALU.is_ge, fill=0.0, base=RUNS - 1,
                               pattern=[[RUNS, EXPERTS]], channel_multiplier=-1).then_inc(pool_set, 1)
            pool.wait_ge(pool_set, 20)
            pool.engine_nop().then_inc(consts, 1)

            pool.wait_ge(bias_ok, 1)
            pool.tensor_tensor(x_bias[:], x_sb[:], out_bias[:, None, :].to_broadcast((P, TILES, P)), ALU.add).then_inc(xbias_ok, 1)
            pool.memset(pad_rows[:], 0).then_inc(pool_set, 1)
            pool.wait_ge(pool_set, 21)
            pool.memset(pad_rows[:, :, TARGET:TARGET + 1], NO_TARGET).then_inc(pads_set, 1)

            def rstd_of(g):
                pool.wait_ge(var2_ok, g + 1)
                pool.tensor_tensor(rstd2[:, group(g)], var_eps2[:, group(g)], minus_half[:, group(g)], ALU.pow).then_inc(rstd2_ok, 1)

            for step in range(STEPS):
                for g in range(GROUPS):
                    stage = step - SKEW * g
                    if stage == CENTRED_T:
                        rstd_of(g)
                    elif stage == SEND:
                        send(pool, g)
            pool.wait_ge(pads_ok, 1)
            pool.indirect_dma_start(rows_dram.rearrange("s (c one) -> (s c) one", one=1),
                                    bass.IndirectOffsetOnAxis(ap=pad_slot[:], axis=0),
                                    pad_rows[:].rearrange("p r c -> p (r c)"), None).then_inc(filled, 16)

            limit = pool.to_reg(SLOTS - 1)
            for t in range(N_TILES):
                pool.wait_ge(y_ok, t + 1)
                for r in range(HALVES):
                    pool.indirect_dma_start(results_dram, bass.IndirectOffsetOnAxis(ap=aims[:].bitcast(U32)[:, t, r, 0:1], axis=0),
                                            y_sb[:, t, r, :], None, bounds_check=limit,
                                            oob_is_err=False).then_inc(scattered, 16)

        @block.scalar
        def _(act):
            act.dma_start(wp[:], wpack).then_inc(ld_w, 16)
            act.wait_ge(ld_w, 16)
            act.activation(tanhs[:], wp[:, GX:GF + 1], ACT.Tanh).then_inc(tanh_ok, 1)
            act.wait_ge(fused_ps, 1)
            act.activation(fused[:, 0:P], once[:, 0:P], ACT.Copy)
            act.wait_ge(tanh_ok, 1)
            act.activation(fused[:, P:2 * P], once[:, P:2 * P], ACT.Copy, scale=tanhs[:, 0:1])
            act.activation(fused[:, 2 * P:3 * P + 1], once[:, 2 * P:3 * P + 1], ACT.Copy).then_inc(fused_ok, 1)

            for h in range(2):
                act.wait_ge(v_ps, h + 1)
                act.activation(v_sb[:, h * HALF:(h + 1) * HALF, 0:P], v_bank[h][:, :].rearrange("p (t d) -> p t d", d=P),
                               ACT.Copy).then_inc(v_ok, 1)

            def tokens(g):
                return slice(g * GROUP * P, (g + 1) * GROUP * P)

            def copy_nt(g):
                act.wait_ge(xnt_ps, g + 1)
                act.activation(xn_t[:, tokens(g)], xnt_bank[:, 0:GROUP * P], ACT.Copy).then_inc(xnt_ok, 1)

            def copy_q(g):
                act.wait_ge(q_ps, g + 1)
                act.activation(q_t[:, tokens(g)], q_bank[:, 0:GROUP * P], ACT.Identity,
                               bias=fused[:, 2 * P:2 * P + 1]).then_inc(q_ok, 1)

            def exp_scores(g):
                act.wait_ge(sub_ok, g + 1)
                for h in range(2):
                    half = slice(h * SEQ, (h + 1) * SEQ)
                    act.activation(probs[half, group(g), half], s_sub[half, g, :, :], ACT.Exp,
                                   scale=SCORE_SCALE).then_inc(prob_ok, 1)

            def copy_pt(g):
                act.wait_ge(pt_ps, g + 1)
                act.activation(p_t[:, g, :], probs_bank[g % 2][:, 0:GROUP * P], ACT.Copy).then_inc(pt_ok, 1)

            def copy_ct(g):
                act.wait_ge(ct_ps, g + 1)
                act.activation(centred_t[:, g, :], turn[g % 2][:, 0:GROUP * P], ACT.Copy).then_inc(ct_ok, 1)

            def high_part(g):
                act.wait_ge(rstd2_ok, g + 1)
                for t in range(g * GROUP, (g + 1) * GROUP):
                    act.activation(row_parts[:, t, :, 0:P], centred[:, t, None, :].to_broadcast((P, TOP_K, P)), ACT.Copy,
                                   scale=rstd2[:, t:t + 1]).then_inc(hi_ok, 1)

            def exp_logits(g):
                act.wait_ge(shift_ok, g + 1)
                act.activation(exps[:, group(g), :], shifted[:, group(g), :], ACT.Exp).then_inc(exps_ok, 1)

            def weights_hi(to, at, loaded_all, made, i):
                act.wait_ge(loaded_all, 16)
                q = experts_of(i)
                act.activation(to[:, q], at[:, q], ACT.Copy, scale=WSCALE).then_inc(made, 1)

            act.wait_ge(probs_zero, 1)
            for step in range(STEPS):
                for g in range(GROUPS):
                    stage = step - SKEW * g
                    if stage == COPY_NORM_T:
                        copy_nt(g)
                    elif stage == COPY_QUERIES:
                        copy_q(g)
                    elif stage == EXPONENT:
                        exp_scores(g)
                    elif stage == COPY_PROBS_T:
                        copy_pt(g)
                    elif stage == COPY_CENTRED_T:
                        copy_ct(g)
                        high_part(g)
                    elif stage == RANKS:
                        exp_logits(g)
                if step in W1_STEPS:
                    weights_hi(w1_hi, w1_sb, ld_w1, w1hi_ok, W1_STEPS.index(step))
                if step in W2_STEPS:
                    weights_hi(w2_hi, w2_sb, ld_w2, w2hi_ok, W2_STEPS.index(step))

            b1 = wp[:, B1:B1 + EXPERTS * BLOCKS].rearrange("p (e b) -> p e b", b=BLOCKS)

            def gelu(t, s, first=False):
                e = act.value_load(tile_experts[0:1, bass.ds(t, 1)], min_val=0, max_val=EXPERTS - 1)
                if not first:
                    act.wait_ge(y_in_ps, t - 1)
                for b in range(BLOCKS):
                    if b % 2 == 0:
                        act.wait_ge(hid_in_ps, 2 * t + b // 2 + 1)
                    psum = hid_ps[s][b // 2][:, b % 2 * SLOT_TILE:(b % 2 + 1) * SLOT_TILE]
                    act.activation(hid[:, s, b, :], psum, ACT.Gelu_apprx_tanh, bias=b1[:, bass.ds(e, 1), b:b + 1],
                                   scale=1.0 / WSCALE).then_inc(hid_ok, 1)
                    if b % 2:
                        act.wait_ge(hid_ok, BLOCKS * t + b + 1)
                        act.activation(hid_hi[:, s, b - 1:b + 1, :], hid[:, s, b - 1:b + 1, :], ACT.Copy).then_inc(hid_hi_ok, 1)

            act.wait_ge(table_ok, 1)
            gelu(0, 0, True)
            gelu(1, 1, True)
            with act.Fori(1, N_TILES // 2) as k:
                gelu(2 * k, 0)
                gelu(2 * k + 1, 1)
            gelu(N_TILES - 1, 0)

        @block.tensor
        def _(pe):
            pe.wait_ge(ld_w, 16)
            pe.wait_ge(dve_set, 1)
            ps = once
            pe.matmul(ps[:, 0:P], wp[:, WQ:WQ + P], wp[:, WK:WK + P], start=True, stop=True)
            pe.matmul(ps[:, P:2 * P], wp[:, WV:WV + P], wp[:, WOT:WOT + P], start=True, stop=True)
            pe.matmul(ps[:, 2 * P:2 * P + 1], wp[:, WK:WK + P], wp[:, BQ:BQ + 1], start=True, stop=True)
            pe.matmul(ps[:, 2 * P + 1:3 * P + 1], out_bias[:], wp[:, WOT:WOT + P], start=True, stop=True).then_inc(fused_ps, 1)

            def values(h):
                if h == 0:
                    pe.wait_ge(ld_ctx, 16)
                for j in range(HALF):
                    t = h * HALF + j
                    mm = pe.matmul(v_bank[h][:, j * P:(j + 1) * P], ctx_sb[:, t * P:(t + 1) * P], fused[:, P:2 * P],
                                   start=True, stop=True)
                mm.then_inc(v_ps, 1)

            def norm_t(g):
                pe.wait_ge(xn_ok, (g + 1) * GROUP)
                if g:
                    pe.wait_ge(xnt_ok, g)
                for j in range(GROUP):
                    mm = pe.transpose(xnt_bank[:, j * P:(j + 1) * P], xn[:, g * GROUP + j, :], ident[:])
                mm.then_inc(xnt_ps, 1)

            def queries(g):
                pe.wait_ge(xnt_ok, g + 1)
                if g:
                    pe.wait_ge(q_ok, g)
                pe.matmul(q_bank[:, 0:GROUP * P], fused[:, 0:P], xn_t[:, g * GROUP * P:(g + 1) * GROUP * P],
                          start=True, stop=True).then_inc(q_ps, 1)

            def scores(g):
                pe.wait_ge(q_ok, g + 1)
                if g >= 2:
                    pe.wait_ge(var2_ok, g - 1)
                for j in range(GROUP):
                    for h in range(2):
                        at = (g * GROUP + j) * P + h * SEQ
                        mm = pe.matmul(score[g % 2][h * SEQ:(h + 1) * SEQ, j * SEQ:(j + 1) * SEQ],
                                       q_t[:, at:at + SEQ], ctx_sb[:, at:at + SEQ],
                                       start=True, stop=True)
                mm.then_inc(s_ps, 1)

            def probs_t(g):
                pe.wait_ge(prob_ok, 2 * (g + 1))
                if g >= 2:
                    pe.wait_ge(pt_ok, g - 1)
                for j in range(GROUP):
                    mm = pe.transpose(probs_bank[g % 2][:, j * P:(j + 1) * P], probs[:, g * GROUP + j, :], ident[:])
                mm.then_inc(pt_ps, 1)

            def attend(g):
                pe.wait_ge(pt_ok, g + 1)
                if g == 0:
                    pe.wait_ge(v_ok, 2)
                    pe.wait_ge(v_ones, 1)
                for j in range(GROUP):
                    mm = pe.matmul(score[g % 2][:, j * (P + 1):(j + 1) * (P + 1)], p_t[:, g, j * P:(j + 1) * P],
                                   v_sb[:, g * GROUP + j, :], start=True, stop=True)
                mm.then_inc(o_ps, 1)

            def centred_turn(g):
                pe.wait_ge(centred_ok, g + 1)
                if g >= 2:
                    pe.wait_ge(group_done, g - 1)
                for j in range(GROUP):
                    mm = pe.transpose(turn[g % 2][:, j * P:(j + 1) * P], centred[:, g * GROUP + j, :], ident[:])
                mm.then_inc(ct_ps, 1)

            def route(g):
                pe.wait_ge(ct_ok, g + 1)
                for j in range(GROUP):
                    at = LOGIT + j * EXPERTS
                    mm = pe.matmul(turn[g % 2][:, at:at + EXPERTS], centred_t[:, g, j * P:(j + 1) * P],
                                   wp[:, GATEW:GATEW + EXPERTS], start=True, stop=True)
                mm.then_inc(logit_ps, 1)

            def ranks(g):
                pe.wait_ge(chosen_ok, g + 1)
                if g == 0:
                    pe.wait_ge(consts, 1)
                for j in range(GROUP):
                    t = g * GROUP + j
                    at = RANK + j * EXPERTS
                    mm = pe.matmul(turn[g % 2][:, at:at + EXPERTS], before[:], chosen[:, t, :], start=True, stop=t == 0)
                    for u in range(t):
                        mm = pe.matmul(turn[g % 2][:, at:at + EXPERTS], ones[:], chosen[:, u, :], start=False, stop=u == t - 1)
                mm.then_inc(rank_ps, 1)

            pe.wait_ge(fused_ok, 1)
            for h in range(2):
                values(h)
            pe.wait_ge(ident_ok, 1)
            for step in range(STEPS):
                for g in range(GROUPS):
                    stage = step - SKEW * g
                    if stage == NORM_T:
                        norm_t(g)
                    elif stage == QUERIES:
                        queries(g)
                    elif stage == SCORES:
                        scores(g)
                    elif stage == PROBS_T:
                        probs_t(g)
                    elif stage == ATTEND:
                        attend(g)
                    elif stage == CENTRED_T:
                        centred_turn(g)
                    elif stage == ROUTE:
                        route(g)
                    elif stage == RANKS:
                        ranks(g)
            for t in range(TILES):
                mm = pe.matmul(xnt_bank[:, COUNT:COUNT + EXPERTS], ones[:], chosen[:, t, :],
                               start=t == 0, stop=t == TILES - 1)
            mm.then_inc(count_ps, 1)

            def expert_of(t):
                return pe.value_load(tile_experts[0:1, t:t + 1], min_val=0, max_val=EXPERTS - 1)

            def turn_rows(t):
                s = t % 2
                pe.wait_ge(loaded[s], 16 * (t // 2 + 1))
                if t >= 2:
                    pe.wait_ge(xs_ok, t - 1)
                to = xs_ps[s][:, :].bitcast(F16)
                for r in range(HALVES):
                    pe.transpose(to[:, r * P:(r + 1) * P], in_parts[:, s, r, 0:P], ident16[:])
                for r in range(HALVES):
                    mm = pe.transpose(to[:, SLOT_TILE + r * P:SLOT_TILE + (r + 1) * P], in_parts[:, s, r, P:2 * P], ident16[:])
                mm.then_inc(xs_in_ps, 1)

            def hidden(t, e):
                s = t % 2
                pe.wait_ge(xs_ok, t + 1)
                if t >= 2:
                    pe.wait_ge(hid_ok, BLOCKS * (t - 1))
                hi, lo = xs_t[:, s, 0, :], xs_t[:, s, 1, :]
                for b in range(BLOCKS):
                    to = hid_ps[s][b // 2][:, b % 2 * SLOT_TILE:(b % 2 + 1) * SLOT_TILE]
                    pe.matmul(to, w1_hi[:, bass.ds(e, 1), b * P:(b + 1) * P], hi, start=True, stop=False)
                    pe.matmul(to, w1_hi[:, bass.ds(e, 1), b * P:(b + 1) * P], lo, start=False, stop=False)
                    mm = pe.matmul(to, w1_lo[:, bass.ds(e, 1), b * P:(b + 1) * P], hi, start=False, stop=True)
                    if b % 2:
                        mm.then_inc(hid_in_ps, 1)

            def output(t, e):
                s = t % 2
                pe.wait_ge(hid_hi_ok, 2 * (t + 1))
                if t:
                    pe.wait_ge(y_ok, t)
                for r in range(HALVES):
                    pe.matmul(y_ps[r][:, 0:P], out_sel[:], b2_16[:, bass.ds(e, 1), :], start=True, stop=False)
                for b in range(BLOCKS):
                    for r in range(HALVES):
                        pe.matmul(y_ps[r][:, 0:P], hid_hi[:, s, b, r * P:(r + 1) * P], w2_lo[:, bass.ds(e, 1), b * P:(b + 1) * P],
                                  start=False, stop=False)
                for b in range(BLOCKS):
                    if b % 2 == 0:
                        pe.wait_ge(hid_lo_ok, 2 * t + b // 2 + 1)
                    for r in range(HALVES):
                        pe.matmul(y_ps[r][:, 0:P], hid_hi[:, s, b, r * P:(r + 1) * P], w2_hi[:, bass.ds(e, 1), b * P:(b + 1) * P],
                                  start=False, stop=False)
                        mm = pe.matmul(y_ps[r][:, 0:P], hid_lo[:, s, b, r * P:(r + 1) * P], w2_hi[:, bass.ds(e, 1), b * P:(b + 1) * P],
                                       start=False, stop=b == BLOCKS - 1)
                mm.then_inc(y_in_ps, 1)

            pe.wait_ge(row_ok, GROUPS)
            pe.wait_ge(table_ok, 1)
            experts = [expert_of(t) for t in range(AHEAD)]
            pe.wait_ge(w1_ok, GROUPS)
            pe.wait_ge(w2_ok, GROUPS)
            pe.wait_ge(b2_ok, 1)
            turn_rows(0)
            for t in range(N_TILES):
                if t + 1 < N_TILES:
                    turn_rows(t + 1)
                hidden(t, experts[t])
                if len(experts) < N_TILES:
                    experts.append(expert_of(len(experts)))
                if t:
                    output(t - 1, experts[t - 1])
            output(N_TILES - 1, experts[N_TILES - 1])

        @block.vector
        def _(v):
            done = 0

            def then(instruction):
                nonlocal done
                instruction.then_inc(dve, 1)
                done += 1
                return done

            v.memset(b2_in[:], 0.0).then_inc(zeroed, 1)
            v.memset(ones[:], 1.0)
            v.memset(v_sb[:, :, P:P + 1], 1.0).then_inc(v_ones, 1)
            then(v.memset(b2_16[:], 0.0))
            v.wait_ge(ld_w, 16)
            v.tensor_copy(out_bias[:], wp[:, BV:BV + 1].to_broadcast((P, P))).then_inc(dve_set, 1)

            for i in range(2):
                tiles = range(i * HALF, (i + 1) * HALF)
                v.wait_ge(ld_x[i], 16)
                for t in tiles:
                    n = then(v.bn_stats(stats[:, t, :], x_sb[:, t, :]))
                v.wait_ge(dve, n)
                for t in tiles:
                    n = then(v.bn_aggr(meanvar[:, t, :], stats[:, t, :]))
                v.wait_ge(dve, n)
                h = slice(i * HALF, (i + 1) * HALF)
                v.tensor_scalar(var_eps[:, h], meanvar[:, h, 1], EPS, None, ALU.add).then_inc(var_ok, 1)
            for t in range(TILES):
                v.wait_ge(rstd_ok, t // HALF + 1)
                v.tensor_scalar(xn[:, t, :], x_sb[:, t, :], meanvar[:, t, 0:1], rstd[:, t:t + 1],
                                ALU.subtract, ALU.mult).then_inc(xn_ok, 1)
            v.wait_ge(fused_ok, 1)
            n = then(v.tensor_tensor(out_bias[:], fused[:, 2 * P + 1:3 * P + 1], wp[:, BO:BO + P], ALU.add))
            v.wait_ge(dve, n)
            v.wait_ge(tanh_ok, 1)
            then(v.tensor_scalar(gate_scale[:], tanhs[:, 1:2], 1.0 / WSCALE, None, ALU.mult))
            v.tensor_scalar(out_bias[:], out_bias[:], tanhs[:, 0:1], None, ALU.mult).then_inc(bias_ok, 1)
            v.wait_ge(consts, 1)
            then(v.tensor_copy(region[:], region_i[:]))
            then(v.tensor_copy(tile_no[:], tile_i[:]))
            then(v.tensor_copy(edge[:], edge_i[:]))
            then(v.tensor_copy(run_from[:], run_i[:]))
            made = then(v.tensor_copy(rows[:, :, :, TARGET], target[:]))

            def score_max(g):
                s = score[g % 2][:, 0:GROUP * SEQ].rearrange("p (j s) -> p j s", j=GROUP)
                v.wait_ge(s_ps, g + 1)
                n = then(v.tensor_reduce(s_max[:, g, :], s, AX_X, ALU.max))
                v.wait_ge(dve, n)
                v.tensor_tensor(s_sub[:, g, :, :], s, s_max[:, g, :, None].to_broadcast((P, GROUP, SEQ)),
                                ALU.subtract).then_inc(sub_ok, 1)

            def residual(g):
                attended = score[g % 2][:, 0:GROUP * (P + 1)].rearrange("p (j c) -> p j c", j=GROUP)
                v.wait_ge(o_ps, g + 1)
                n = then(v.reciprocal(rden[:, g, :], attended[:, :, P]))
                v.wait_ge(dve, n)
                v.wait_ge(xbias_ok, 1)
                for j in range(GROUP):
                    t = g * GROUP + j
                    n = then(v.scalar_tensor_tensor(x1[:, t, :], attended[:, j, 0:P], rden[:, g, j:j + 1],
                                                    x_bias[:, t, :], ALU.mult, ALU.add))
                v.wait_ge(dve, n)
                for t in range(g * GROUP, (g + 1) * GROUP):
                    n = then(v.bn_stats(stats2[:, t, :], x1[:, t, :]))
                v.wait_ge(dve, n)
                for t in range(g * GROUP, (g + 1) * GROUP):
                    n = then(v.bn_aggr(meanvar2[:, t, :], stats2[:, t, :]))
                v.wait_ge(dve, n)
                v.tensor_scalar(var_eps2[:, group(g)], meanvar2[:, group(g), 1], EPS, None, ALU.add).then_inc(var2_ok, 1)
                for t in range(g * GROUP, (g + 1) * GROUP):
                    m = v.tensor_scalar(centred[:, t, :], x1[:, t, :], meanvar2[:, t, 0:1], None, ALU.subtract)
                m.then_inc(centred_ok, 1)

            def choose(g):
                v.wait_ge(logit_ps, g + 1)
                v.wait_ge(rstd2_ok, g + 1)
                n = then(v.tensor_tensor(logits[:, group(g), :], turn[g % 2][:, LOGIT:LOGIT + GROUP * EXPERTS].rearrange(
                    "p (j e) -> p j e", j=GROUP), rstd2[:, group(g), None].to_broadcast((P, GROUP, EXPERTS)), ALU.mult))
                v.wait_ge(dve, n)
                for t in range(g * GROUP, (g + 1) * GROUP):
                    n = then(v.max(sorted_l[:, t, :], logits[:, t, :]))
                v.wait_ge(dve, n)
                for t in range(g * GROUP, (g + 1) * GROUP):
                    n = then(v.max_index(index[:, t, :], sorted_l[:, t, :], logits[:, t, :]))
                v.tensor_tensor(shifted[:, group(g), :], sorted_l[:, group(g), :],
                                sorted_l[:, group(g), 0:1].to_broadcast((P, GROUP, EXPERTS)), ALU.subtract).then_inc(shift_ok, 1)
                v.wait_ge(dve, n)
                n = then(v.tensor_tensor(choice[:, group(g), :, :], iota_i[:, None, None, :].to_broadcast((P, GROUP, TOP_K, EXPERTS)),
                                         index[:, group(g), 0:TOP_K, None].to_broadcast((P, GROUP, TOP_K, EXPERTS)), ALU.is_equal))
                v.wait_ge(dve, n)
                v.tensor_tensor(chosen[:, group(g), :], choice[:, group(g), 0, :], choice[:, group(g), 1, :],
                                ALU.add).then_inc(chosen_ok, 1)

            def low_parts(g):
                for t in range(g * GROUP, (g + 1) * GROUP):
                    v.wait_ge(hi_ok, t + 1)
                    then(v.scalar_tensor_tensor(row_parts[:, t, :, P:2 * P], centred[:, t, None, :].to_broadcast((P, TOP_K, P)),
                                                rstd2[:, t:t + 1], row_parts[:, t, :, 0:P], ALU.mult, ALU.subtract))

            def fill_rows_of(g):
                v.wait_ge(exps_ok, g + 1)
                n = then(v.tensor_reduce(exp_sum[:, group(g)], exps[:, group(g), :], AX_X, ALU.add))
                v.wait_ge(dve, n)
                n = then(v.reciprocal(exp_rec[:, group(g)], exp_sum[:, group(g)]))
                v.wait_ge(dve, n)
                then(v.scalar_tensor_tensor(rows[:].bitcast(F32)[:, group(g), :, GATE], exps[:, group(g), 0:TOP_K], gate_scale[:, 0:1],
                                            exp_rec[:, group(g), None].to_broadcast((P, GROUP, TOP_K)), ALU.mult, ALU.mult))
                v.wait_ge(rank_ps, g + 1)
                v.tensor_tensor(place[:, group(g), :], turn[g % 2][:, RANK:RANK + GROUP * EXPERTS].rearrange("p (j e) -> p j e", j=GROUP),
                                region[:, None, :].to_broadcast((P, GROUP, EXPERTS)), ALU.add).then_inc(group_done, 1)
                v.wait_ge(group_done, g + 1)
                n = then(v.tensor_tensor(place_k[:, group(g), :, :], choice[:, group(g), :, :],
                                         place[:, group(g), None, :].to_broadcast((P, GROUP, TOP_K, EXPERTS)), ALU.mult))
                v.wait_ge(dve, n)
                n = then(v.tensor_reduce(slot_f[:, group(g), :], place_k[:, group(g), :, :], AX_X, ALU.add))
                v.wait_ge(dve, n)
                v.tensor_copy(slot[:, TOP_K * g * GROUP:TOP_K * (g + 1) * GROUP],
                              slot_f[:, group(g), :].rearrange("p t k -> p (t k)")).then_inc(row_ok, 1)

            def weights_lo(to, at, hi, hi_made, made_lo, i):
                q = experts_of(i)
                v.wait_ge(hi_made, i + 1)
                v.scalar_tensor_tensor(to[:, q, :], at[:, q, :], WSCALE, hi[:, q, :], ALU.mult, ALU.subtract).then_inc(made_lo, 1)

            v.wait_ge(dve, made)
            for step in range(STEPS):
                for g in range(GROUPS):
                    stage = step - SKEW * g
                    if stage == MAXIMUM:
                        score_max(g)
                    elif stage == RESIDUAL:
                        residual(g)
                    elif stage == ROUTE:
                        low_parts(g)
                    elif stage == CHOOSE:
                        choose(g)
                    elif stage == FILL:
                        fill_rows_of(g)
                if step in W1_STEPS:
                    weights_lo(w1_lo, w1_sb, w1_hi, w1hi_ok, w1_ok, W1_STEPS.index(step))
                if step in W2_LO_STEPS:
                    weights_lo(w2_lo, w2_sb, w2_hi, w2hi_ok, w2_ok, W2_LO_STEPS.index(step))

            v.wait_ge(count_ps, 1)
            then(v.tensor_copy(counts[:], xnt_bank[0:1, COUNT:COUNT + EXPERTS]))
            n = then(v.tensor_tensor(run_row[:], xnt_bank[:, COUNT:COUNT + EXPERTS], run_from[:], ALU.add))
            v.wait_ge(dve, n)
            then(v.tensor_tensor(run_word[:], run_row[:], run_sel[:], ALU.mult))
            n = then(v.tensor_tensor(over[:], counts[:, :, None].to_broadcast((1, EXPERTS, EDGES)), edge[:], ALU.is_gt))
            v.wait_ge(dve, n)
            then(v.tensor_reduce(pad_at[:], run_word[:], AX_X, ALU.add))
            n = then(v.tensor_reduce(n_tiles[:], over[:], AX_X, ALU.add))
            v.wait_ge(dve, n)
            v.tensor_copy(pad_slot[:], pad_at[:]).then_inc(pads_ok, 1)
            n = then(v.tensor_tensor(upto_n[:], upto[:], n_tiles[:, None, :].to_broadcast((1, EXPERTS, EXPERTS)), ALU.mult))
            v.wait_ge(dve, n)
            n = then(v.tensor_reduce(ends[:], upto_n[:], AX_X, ALU.add))
            v.wait_ge(dve, n)
            n = then(v.tensor_tensor(past[:], tile_no[:], ends[:, None, :].to_broadcast((1, N_TILES, EXPERTS)), ALU.is_ge))
            v.wait_ge(dve, n)
            then(v.tensor_reduce(tile_e[:], past[:], AX_X, ALU.add))
            n = then(v.tensor_tensor(past_n[:], past[:], n_tiles[:, None, :].to_broadcast((1, N_TILES, EXPERTS)), ALU.mult))
            v.wait_ge(dve, n)
            n = then(v.tensor_reduce(tile_base[:], past_n[:], AX_X, ALU.add))
            v.wait_ge(dve, n)
            then(v.tensor_scalar(tile_experts[:], tile_e[:], float(EXPERTS - 1), None, ALU.min))
            n = then(v.tensor_tensor(tile_row[:], tile_no[:, :, 0], tile_base[:], ALU.subtract))
            v.wait_ge(dve, n)
            n = then(v.tensor_scalar(tile_row2[:], tile_e[:], float(REGION // SLOT_TILE), None, ALU.mult))
            v.wait_ge(dve, n)
            n = then(v.tensor_tensor(tile_base[:], tile_row[:], tile_row2[:], ALU.add))
            v.wait_ge(dve, n)
            v.tensor_scalar(tile_rows[:], tile_base[:], float(SLOT_TILE), float(PAD_ROW), ALU.mult, ALU.min).then_inc(table_ok, 1)

            for i in range(len(W2_LO_STEPS), GROUPS):
                weights_lo(w2_lo, w2_sb, w2_hi, w2hi_ok, w2_ok, i)
            v.wait_ge(ld_b, 32)
            n = then(v.tensor_scalar(b2_hi[:], b2_in[:], WSCALE, None, ALU.mult))
            v.wait_ge(dve, n)
            parts = b2_16[:].rearrange("p e f -> p (e f)")
            v.scalar_tensor_tensor(parts[32:33, :], b2_in[32:33, :], WSCALE, b2_hi[32:33, :], ALU.mult, ALU.subtract)
            v.tensor_copy(parts[0:1, :], b2_hi[0:1, :]).then_inc(b2_ok, 1)

            def copy_rows(t, s, first=False):
                v.wait_ge(xs_in_ps, t + 1)
                if not first:
                    v.wait_ge(hid_in_ps, t - 1)
                v.tensor_copy(xs_t[:, s, :, :], xs_ps[s][:, :].bitcast(F16)[:, 0:2 * SLOT_TILE].rearrange("p (c s) -> p c s", c=2)).then_inc(xs_ok, 1)
                v.tensor_copy(aims[:, t, :, :], in_rows[:, s, :, TARGET:GATE + 1]).then_inc(row_read, 1)

            def low_part(t, s, first=False):
                if not first:
                    v.wait_ge(y_in_ps, t - 1)
                for i in range(2):
                    v.wait_ge(hid_hi_ok, 2 * t + i + 1)
                    b = slice(2 * i, 2 * i + 2)
                    v.tensor_tensor(hid_lo[:, s, b, :], hid[:, s, b, :], hid_hi[:, s, b, :], ALU.subtract).then_inc(hid_lo_ok, 1)

            def gated(t, s):
                v.wait_ge(y_in_ps, t + 1)
                v.wait_ge(row_read, t + 1)
                for r in range(HALVES):
                    m = v.tensor_scalar(y_sb[:, t, r, :], y_ps[r][:, 0:P], aims[:].bitcast(F32)[:, t, r, 1:2], None, ALU.mult)
                m.then_inc(y_ok, 1)

            copy_rows(0, 0, True)
            copy_rows(1, 1, True)
            for t in range(N_TILES):
                low_part(t, t % 2, t < 2)
                if t + 2 < N_TILES:
                    copy_rows(t + 2, t % 2)
                gated(t, t % 2)

            for i in range(4):
                q = slice(2 * i, 2 * i + 2)
                v.wait_ge(ld_res[i], 16)
                n = then(v.tensor_tensor(out_sb[:, q, :], x1[:, q, :], res[:, q, 0, :], ALU.add))
                v.wait_ge(dve, n)
                v.tensor_tensor(out_sb[:, q, :], out_sb[:, q, :], res[:, q, 1, :], ALU.add).then_inc(out_ok, 1)


def kernel(**inputs):
    import numpy as np
    import concourse.bacc as bacc
    from concourse.bass_utils import run_bass_kernel_spmd

    a = {name: np.asarray(value) for name, value in inputs.items()}
    wide = [a["L0_xattn_Wq"], a["L0_xattn_Wk"], a["L0_xattn_Wv"], a["L0_xattn_Wo"].T, a["L0_ffn_gate_w"].T,
            a["L0_xattn_bq"][:, None], a["L0_xattn_bv"][:, None],
            np.broadcast_to(a["L0_xattn_bo"][None, :], (P, P)),
            np.broadcast_to(a["g_xattn"][None, :], (P, 1)), np.broadcast_to(a["g_ffn"][None, :], (P, 1)),
            a["L0_ffn_b1"].reshape(EXPERTS * BLOCKS, P).T]
    arrays = {
        "x": a["x"].reshape(TOKENS, P),
        "ctx_t": a["ctx_1024"].reshape(TOKENS, P).T,
        "wpack": np.concatenate(wide, axis=1),
        "b2": a["L0_ffn_b2"].reshape(1, EXPERTS * P),
        "w1": a["L0_ffn_w1"].transpose(2, 1, 0),
        "w2": a["L0_ffn_w2"].reshape(P, EXPERTS, BLOCKS, P).transpose(3, 1, 2, 0).reshape(P, EXPERTS, FF),
    }
    arrays = {f"in_{name}": np.ascontiguousarray(value) for name, value in arrays.items()}

    nc = bacc.Bacc("TRN2", target_bir_lowering=False, num_devices=1)
    args = [nc.dram_tensor(name, value.shape, mybir.dt.from_np(value.dtype), kind="ExternalInput").ap()
            for name, value in arrays.items()]
    out = nc.dram_tensor("out", (TOKENS, P), F32, kind="ExternalOutput").ap()
    gated_block(nc, *args, out)
    result = run_bass_kernel_spmd(nc, [arrays], core_ids=[0])
    return result.results[0]["out"].reshape(BATCH, SEQ, P)
```

```python
from contextlib import ExitStack

import concourse.bass as bass
from concourse import mybir

ALU = mybir.AluOpType
ACT = mybir.ActivationFunctionType
AX_X = mybir.AxisListType.X
F32, F16, BF16 = mybir.dt.float32, mybir.dt.float16, mybir.dt.bfloat16
I32, U32 = mybir.dt.int32, mybir.dt.uint32

P = 128
BATCH, SEQ = 16, 64
TOKENS = BATCH * SEQ
TILES = TOKENS // P
SIZES = [2, 2, 2, 2]
GROUPS = len(SIZES)
STARTS = [sum(SIZES[:g]) for g in range(GROUPS + 1)]
PIECES = [(0, 2), (2, 4), (4, 8)]
PARTS = 4
EXPERTS, TOP_K, FF = 8, 2, 512
BLOCKS = FF // P
SLOTS = TOP_K * TOKENS
HALVES = 2
SLOT_TILE = HALVES * P
EDGES = TOKENS // SLOT_TILE
REGION = TOKENS + SLOT_TILE
RUNS = P // EXPERTS
PAD_RUN = SLOT_TILE // RUNS
PAD_ROW = EXPERTS * REGION
N_TILES = (SLOTS - EXPERTS) // SLOT_TILE + EXPERTS
CLOCK_START, CLOCK_ROWS = 6, 8
ROW_BUFFERS = 3
AHEAD = 8
ROW = P + 2
TARGET, GATE = P, P + 1
NO_TARGET = 4 * SLOTS
EPS = 1e-5
WSCALE = 16.0
SCORE_SCALE = float(P) ** -0.5
(NORM_T, COPY_NORM_T, QUERIES, COPY_QUERIES, SCORES, MAXIMUM, EXPONENT, PROBS_T, COPY_PROBS_T, ATTEND, RESIDUAL, RSTD2,
 CENTRE, CENTRED_T, COPY_CENTRED_T, HIGH, ROUTE, CHOOSE, LOW, RANKS, EXP_LOGITS, TWICE, FILL, SEND) = range(24)
W1_HIGH, W2_HIGH, W1_LOW, W2_LOW = range(24, 28)
VALUES, COPY_VALUES, BIASES, NUMBERS = range(28, 32)
TIMES = [-1.2, -0.2, 2.2, 3.0, 4.0, 5.8, 5.2, 5.0, 7.2, 6.9, 9.2, 9.0,
         10.7, 10.8, 10.9, 11.7, 11.1, 14.4, 14.9, 15.5, 13.6, 15.7, 15.8, 15.9]
OFFSETS = [0, 2.7, 6.0, 8.7]
PART_TIMES = [[7.2, 14.1, 16.1, 23.1], [21.1, 26.6, 32.1, 44.1], [33.5, 34.5, 52.0, 56.0], [30.0, 38, 45.0, 46.0],
              [-12.0, 2.7], [2.3, 6.7], [10.5], [6]]
ORDER = sorted([(TIMES[step] + OFFSETS[g], step, g) for step in range(24) for g in range(GROUPS)]
               + [(PART_TIMES[k][i], W1_HIGH + k, i) for k in range(len(PART_TIMES)) for i in range(len(PART_TIMES[k]))])
ORDER = [(step, g) for _, step, g in ORDER]
TABLE = 30
WQ, WK, WV, WOT, GATEW, BQ, BV, BO, GX, GF, B1 = 0, P, 2 * P, 3 * P, 4 * P, 4 * P + 8, 4 * P + 9, 4 * P + 10, 5 * P + 10, 5 * P + 11, 5 * P + 12
WCOLS = B1 + EXPERTS * BLOCKS


def gated_block(nc, x, ctx_t, wpack, b2, w1, w2, out):
    ctx = ExitStack()
    with ctx:
        def sb(name, shape, dt):
            return ctx.enter_context(nc.sbuf_tensor(name, shape, dt))

        def sem(name):
            return ctx.enter_context(nc.semaphore(name))

        rows_dram = nc.dram_tensor("dispatched", [PAD_ROW + SLOT_TILE, ROW], I32, kind="Internal").ap()
        results_dram = nc.dram_tensor("results", [SLOTS, P], F32, kind="Internal").ap()

        ident = sb("ident", [P, P], F32)
        ident16 = sb("ident16", [P, P], F16)
        before = sb("before", [P, P], BF16)
        ones = sb("ones", [P, P], BF16)
        iota_i = sb("iota_i", [P, EXPERTS], I32)
        region_i = sb("region_i", [P, EXPERTS], I32)
        region = sb("region", [P, EXPERTS], F32)
        target = sb("target", [P, TILES, TOP_K], I32)
        pad_rows = sb("pad_rows", [P, PAD_RUN, ROW], I32)
        run_sel = sb("run_sel", [P, EXPERTS], F32)
        run_i = sb("run_i", [P, EXPERTS], I32)
        run_from = sb("run_from", [P, EXPERTS], F32)
        run_row = sb("run_row", [P, EXPERTS], F32)
        run_word = sb("run_word", [P, EXPERTS], F32)
        pad_at = sb("pad_at", [P, 1], F32)
        pad_slot = sb("pad_slot", [P, 1], U32)
        minus_half = sb("minus_half", [P, TILES], F32)
        out_sel = sb("out_sel", [33, P], F16)
        tile_i = sb("tile_i", [1, N_TILES, EXPERTS], I32)
        tile_no = sb("tile_no", [1, N_TILES, EXPERTS], F32)
        edge_i = sb("edge_i", [1, EXPERTS, EDGES], I32)
        edge = sb("edge", [1, EXPERTS, EDGES], F32)
        upto = sb("upto", [1, EXPERTS, EXPERTS], F32)

        x_sb = sb("x_sb", [P, TILES, P], F32)
        ctx_sb = sb("ctx_sb", [P, TOKENS], F32)
        wp = sb("wp", [P, WCOLS], F32)
        b2_in = sb("b2_in", [33, EXPERTS * P], F32)
        w1_sb = sb("w1_sb", [P, EXPERTS, FF], F32)
        w2_sb = sb("w2_sb", [P, EXPERTS, FF], F32)

        w1_hi = sb("w1_hi", [P, EXPERTS, FF], F16)
        w1_lo = sb("w1_lo", [P, EXPERTS, FF], F16)
        w2_hi = sb("w2_hi", [P, EXPERTS, FF], F16)
        w2_lo = sb("w2_lo", [P, EXPERTS, FF], F16)
        b2_hi = sb("b2_hi", [33, EXPERTS * P], F16)
        b2_16 = sb("b2_16", [33, EXPERTS, P], F16)

        fused = sb("fused", [P, 3 * P + 1], F32)
        tanhs = sb("tanhs", [P, 2], F32)
        gelu_first = sb("gelu_first", [P, 2], F32)
        out_bias = sb("out_bias", [P, P], F32)
        x_bias = sb("x_bias", [P, TILES, P], F32)
        stats = sb("stats", [P, TILES, 6], F32)
        meanvar = sb("meanvar", [P, TILES, 2], F32)
        var_eps = sb("var_eps", [P, TILES], F32)
        rstd = sb("rstd", [P, TILES], F32)
        xn = sb("xn", [P, TILES, P], F32)
        xn_t = sb("xn_t", [P, TOKENS], F32)
        q_t = sb("q_t", [P, TOKENS], F32)
        v_sb = sb("v_sb", [P, TILES, P + 1], F32)
        s_max = sb("s_max", [P, TILES], F32)
        s_sub = sb("s_sub", [P, TILES, SEQ], F32)
        probs = sb("probs", [P, TILES, P], F32)
        p_t = sb("p_t", [P, TOKENS], F32)
        rden = sb("rden", [P, TILES], F32)
        neg_x1 = sb("neg_x1", [P, TILES, P], F32)

        stats2 = sb("stats2", [P, TILES, 6], F32)
        meanvar2 = sb("meanvar2", [P, TILES, 2], F32)
        var_eps2 = sb("var_eps2", [P, TILES], F32)
        rstd2 = sb("rstd2", [P, TILES], F32)
        centred = sb("centred", [P, TILES, P], F32)
        centred_t = sb("centred_t", [P, TOKENS], F32)
        logits = sb("logits", [P, TILES, EXPERTS], F32)
        sorted_l = sb("sorted_l", [P, TILES, EXPERTS], F32)
        index = sb("index", [P, TILES, EXPERTS], U32)
        choice = sb("choice", [P, TILES, TOP_K, EXPERTS], F32)
        chosen = sb("chosen", [P, TILES, EXPERTS], BF16)
        shifted = sb("shifted", [P, TILES, EXPERTS], F32)
        exps = sb("exps", [P, TILES, EXPERTS], F32)
        exp_sum = sb("exp_sum", [P, TILES], F32)
        exp_rec = sb("exp_rec", [P, TILES], F32)
        gate_scale = sb("gate_scale", [P, 1], F32)
        place = sb("place", [P, TILES, EXPERTS], F32)
        place_k = sb("place_k", [P, TILES, TOP_K, EXPERTS], F32)
        slot_f = sb("slot_f", [P, TILES, TOP_K], F32)
        slot = sb("slot", [P, TOP_K * TILES], U32)
        rows = sb("rows", [P, TILES, TOP_K, ROW], I32)

        counts = sb("counts", [1, EXPERTS], F32)
        over = sb("over", [1, EXPERTS, EDGES], F32)
        n_tiles = sb("n_tiles", [1, EXPERTS], F32)
        upto_n = sb("upto_n", [1, EXPERTS, EXPERTS], F32)
        ends = sb("ends", [1, EXPERTS], F32)
        past = sb("past", [1, N_TILES, EXPERTS], F32)
        past_n = sb("past_n", [1, N_TILES, EXPERTS], F32)
        tile_e = sb("tile_e", [1, N_TILES], F32)
        tile_base = sb("tile_base", [1, N_TILES], F32)
        tile_row = sb("tile_row", [1, N_TILES], F32)
        tile_row2 = sb("tile_row2", [1, N_TILES], F32)
        tile_rows = sb("tile_rows", [1, N_TILES], I32)
        tile_experts = sb("tile_experts", [1, N_TILES], I32)

        in_rows = sb("in_rows", [P, ROW_BUFFERS, HALVES, ROW], I32)
        xs_t = sb("xs_t", [P, 2, 2, SLOT_TILE], F16)
        hid = sb("hid", [P, 2, BLOCKS, SLOT_TILE], F32)
        hid_hi = sb("hid_hi", [P, 2, BLOCKS, SLOT_TILE], F16)
        hid_lo = sb("hid_lo", [P, 2, BLOCKS, SLOT_TILE], F16)
        y_sb = sb("y_sb", [P, N_TILES, HALVES, P], F32)
        aims = sb("aims", [P, N_TILES, HALVES, 2], I32)

        row_parts, in_parts = rows[:].bitcast(F16), in_rows[:].bitcast(F16)

        res = sb("res", [P, TILES, TOP_K, P], F32)
        out_sb = sb("out_sb", [P, TILES, P], F32)

        bank = [ctx.enter_context(nc.psum_tensor(f"bank{i}", [P, 512], F32)) for i in range(8)]
        v_bank = [bank[1], bank[5]]
        once = bank[0]
        xnt_bank = bank[4]
        q_bank = bank[7]
        turn = [bank[1], bank[5]]
        probs_bank = [bank[2], bank[6]]
        score = [bank[3], bank[0]]
        LOGIT = max(SIZES) * P
        RANK, COUNT = LOGIT + max(SIZES) * EXPERTS, 0
        xs_ps = [bank[0], bank[4]]
        hid_ps = [[bank[1], bank[3]], [bank[5], bank[7]]]
        y_ps = [bank[2], bank[6]]

        chunks = [slice(2 * i, 2 * i + 2) for i in range(4)]
        POOL_CHUNK = 1

        ld_x, ld_ctx, ld_w = [sem(f"ld_x{i}") for i in range(len(PIECES))], sem("ld_ctx"), sem("ld_w")
        ld_b, ld_w1, ld_w2 = sem("ld_b"), sem("ld_w1"), sem("ld_w2")
        pool_set, ident_ok, probs_zero, consts = sem("pool_set"), sem("ident_ok"), sem("probs_zero"), sem("consts")
        dve_set, ones_ok, pads_set, iotas, eps_added = sem("dve_set"), sem("ones_ok"), sem("pads_set"), sem("iotas"), sem("eps_added")
        zeroed = sem("zeroed")
        fused_ps, fused_ok, tanh_ok = sem("fused_ps"), sem("fused_ok"), sem("tanh_ok")
        bias_ok, xbias_ok = sem("bias_ok"), sem("xbias_ok")
        dve = sem("dve")
        var_ok, rstd_ok, xn_ok = sem("var_ok"), sem("rstd_ok"), sem("xn_ok")
        v_ps, v_ok, v_ones = sem("v_ps"), sem("v_ok"), sem("v_ones")
        xnt_ps, xnt_ok, q_ps, q_ok = sem("xnt_ps"), sem("xnt_ok"), sem("q_ps"), sem("q_ok")
        s_ps, sub_ok, prob_ok = sem("s_ps"), sem("sub_ok"), sem("prob_ok")
        pt_ps, pt_ok, o_ps = sem("pt_ps"), sem("pt_ok"), sem("o_ps")
        var2_ok, rstd2_ok, centred_ok = sem("var2_ok"), sem("rstd2_ok"), sem("centred_ok")
        ct_ps, ct_ok, logit_ps = sem("ct_ps"), sem("ct_ok"), sem("logit_ps")
        chosen_ok, rank_ps, shift_ok, exps_ok = sem("chosen_ok"), sem("rank_ps"), sem("shift_ok"), sem("exps_ok")
        hi_ok, lo_ok, twice_ok, row_ok = sem("hi_ok"), sem("lo_ok"), sem("twice_ok"), sem("row_ok")
        group_done = sem("group_done")
        sent = sem("sent")
        padded, pads_ok, filled = sem("padded"), sem("pads_ok"), sem("filled")
        count_ps, table_ok = sem("count_ps"), sem("table_ok")
        w1hi_ok, w1_ok, w2hi_ok, w2_ok, b2_ok = sem("w1hi_ok"), sem("w1_ok"), sem("w2hi_ok"), sem("w2_ok"), sem("b2_ok")
        loaded = [sem(f"loaded{i}") for i in range(ROW_BUFFERS)]
        xs_in_ps, xs_ok, hid_in_ps, hid_hi_ok, hid_ok, hid_lo_ok = sem("xs_in_ps"), sem("xs_ok"), sem("hid_in_ps"), sem("hid_hi_ok"), sem("hid_ok"), sem("hid_lo_ok")
        y_in_ps, y_ok, row_read = sem("y_in_ps"), sem("y_ok"), sem("row_read")
        scattered = sem("scattered")
        ld_res, out_ok, pool_summed, pool_out_ok, stored = [sem(f"ld_res{i}") for i in range(len(chunks))], sem("out_ok"), sem("pool_summed"), sem("pool_out_ok"), sem("stored")

        x_view = x.rearrange("(t p) d -> p t d", p=P)
        out_view = out.rearrange("(t p) d -> p t d", p=P)
        res_view = results_dram.rearrange("(t k p) d -> p t k d", p=P, k=TOP_K)
        HALF = TILES // 2

        def experts_of(i):
            return slice(i * EXPERTS // PARTS, (i + 1) * EXPERTS // PARTS)

        def group(g):
            return slice(STARTS[g], STARTS[g + 1])

        def tiles_of(g):
            return range(STARTS[g], STARTS[g + 1])

        def tokens(g):
            return slice(STARTS[g] * P, STARTS[g + 1] * P)

        block = ctx.enter_context(nc.Block())

        @block.sync
        def _(sp):
            for i, (a, b) in enumerate(PIECES):
                sp.dma_start(x_sb[:, a:b, :], x_view[:, a:b, :]).then_inc(ld_x[i], 16)
            sp.dma_start(ctx_sb[:], ctx_t).then_inc(ld_ctx, 16)
            sp.wait_ge(zeroed, 1)
            for i in range(2):
                sp.dma_start(b2_in[32 * i:32 * i + 1, :], b2).then_inc(ld_b, 16)
            sp.dma_start(w1_sb[:], w1).then_inc(ld_w1, 16)
            sp.dma_start(w2_sb[:], w2).then_inc(ld_w2, 16)
            sp.wait_ge(pads_set, 1)
            sp.dma_start(rows_dram[PAD_ROW:PAD_ROW + SLOT_TILE, :].rearrange("(p r) c -> p r c", r=HALVES), pad_rows[:, 0:HALVES, :]).then_inc(padded, 16)
            sp.wait_ge(table_ok, 1)
            first = [sp.value_load(tile_rows[0:1, t:t + 1], min_val=0, max_val=PAD_ROW) for t in range(ROW_BUFFERS)]
            sp.wait_ge(sent, 16 * SLOTS // P)
            sp.wait_ge(filled, 16)
            sp.wait_ge(padded, 16)

            def load_rows(at, s):
                sp.dma_start(in_rows[:, s, :, :], rows_dram[bass.ds(at, SLOT_TILE), :].rearrange("(p r) c -> p r c", r=HALVES)).then_inc(loaded[s], 16)

            def next_rows(t, s):
                at = sp.value_load(tile_rows[0:1, bass.ds(t, 1)], min_val=0, max_val=PAD_ROW)
                sp.wait_ge(row_read, t - ROW_BUFFERS + 1)
                load_rows(at, s)

            for s in range(ROW_BUFFERS):
                load_rows(first[s], s)
            with sp.Fori(1, N_TILES // ROW_BUFFERS) as k:
                for s in range(ROW_BUFFERS):
                    next_rows(ROW_BUFFERS * k + s, s)
            assert N_TILES % ROW_BUFFERS == 0
            sp.wait_ge(scattered, 16 * HALVES * N_TILES)
            for i, q in enumerate(chunks):
                sp.dma_start(res[:, q, :, :], res_view[:, q, :, :]).then_inc(ld_res[i], 16)
            for i, q in enumerate(chunks):
                if i == POOL_CHUNK:
                    sp.wait_ge(pool_out_ok, 1)
                else:
                    sp.wait_ge(out_ok, i + 1 - (i > POOL_CHUNK))
                sp.dma_start(out_view[:, q, :], out_sb[:, q, :]).then_inc(stored, 16)
            sp.wait_ge(stored, 16 * len(chunks))

        def send(pool, g):
            pool.wait_ge(row_ok, g + 1)
            pool.wait_ge(twice_ok, g + 1)
            for t in tiles_of(g):
                for k in range(TOP_K):
                    j = TOP_K * t + k
                    pool.indirect_dma_start(rows_dram, bass.IndirectOffsetOnAxis(ap=slot[:, j:j + 1], axis=0),
                                            rows[:, t, k, :], None).then_inc(sent, 16)

        @block.gpsimd
        def _(pool):
            pool.memset(ident[:], 0.0).then_inc(pool_set, 1)
            pool.memset(minus_half[:], -0.5).then_inc(pool_set, 1)
            pool.wait_ge(pool_set, 2)
            pool.affine_select(out=ident[:], in_=ident[:], compare_op=ALU.not_equal, fill=1.0, base=0,
                               pattern=[[-1, P]], channel_multiplier=1).then_inc(ident_ok, 1)
            pool.iota(iota_i[:], [[1, EXPERTS]], base=0, channel_multiplier=0).then_inc(iotas, 1)
            pool.iota(region_i[:], [[REGION, EXPERTS]], base=0, channel_multiplier=0).then_inc(iotas, 1)
            pool.iota(target[:], [[TOP_K * P, TILES], [P, TOP_K]], base=0, channel_multiplier=1).then_inc(iotas, 1)
            pool.iota(tile_i[:], [[1, N_TILES], [0, EXPERTS]], base=0, channel_multiplier=0).then_inc(iotas, 1)
            pool.iota(run_i[:], [[REGION - SLOT_TILE, EXPERTS]], base=0, channel_multiplier=PAD_RUN).then_inc(iotas, 1)
            pool.iota(edge_i[:], [[0, EXPERTS], [SLOT_TILE, EDGES]], base=0, channel_multiplier=0).then_inc(iotas, 1)
            pool.memset(probs[:], 0.0).then_inc(probs_zero, 1)
            for m in (ident16, out_sel):
                pool.memset(m[:], 0.0).then_inc(pool_set, 1)
            pool.memset(before[:], 1.0).then_inc(pool_set, 1)
            pool.memset(upto[:], 1.0).then_inc(pool_set, 1)
            pool.memset(run_sel[:], float(ROW)).then_inc(pool_set, 1)
            pool.wait_ge(pool_set, 7)
            pool.affine_select(out=ident16[:], in_=ident16[:], compare_op=ALU.not_equal, fill=1.0, base=0,
                               pattern=[[-1, P]], channel_multiplier=1).then_inc(pool_set, 1)
            pool.affine_select(out=before[:], in_=before[:], compare_op=ALU.is_gt, fill=0.0, base=0,
                               pattern=[[1, P]], channel_multiplier=-1).then_inc(pool_set, 1)
            pool.affine_select(out=upto[:], in_=upto[:], compare_op=ALU.is_ge, fill=0.0, base=0,
                               pattern=[[1, EXPERTS], [-1, EXPERTS]], channel_multiplier=0).then_inc(pool_set, 1)
            pool.affine_select(out=run_sel[:], in_=run_sel[:], compare_op=ALU.is_ge, fill=0.0, base=0,
                               pattern=[[-RUNS, EXPERTS]], channel_multiplier=1).then_inc(pool_set, 1)
            sums = 0

            def root(to, with_eps, variance, power):
                nonlocal sums
                sums += 1
                pool.tensor_scalar(with_eps, variance, EPS, None, ALU.add).then_inc(eps_added, 1)
                pool.wait_ge(eps_added, sums)
                return pool.tensor_tensor(to, with_eps, power, ALU.pow)

            for i, (a, b) in enumerate(PIECES):
                h = slice(a, b)
                pool.wait_ge(var_ok, i + 1)
                root(rstd[:, h], var_eps[:, h], meanvar[:, h, 1], minus_half[:, h]).then_inc(rstd_ok, 1)
            pool.wait_ge(bias_ok, 1)
            pool.tensor_tensor(x_bias[:], out_bias[:, None, :].to_broadcast((P, TILES, P)), x_sb[:], ALU.subtract).then_inc(xbias_ok, 1)
            for i in range(2):
                if i:
                    pool.wait_ge(pool_set, 12)
                pool.affine_select(out=out_sel[:], in_=out_sel[:], compare_op=ALU.not_equal, fill=1.0,
                                   base=-32 * i, pattern=[[0, P]], channel_multiplier=1).then_inc(pool_set, 1)
            pool.affine_select(out=run_sel[:], in_=run_sel[:], compare_op=ALU.is_ge, fill=0.0, base=RUNS - 1,
                               pattern=[[RUNS, EXPERTS]], channel_multiplier=-1).then_inc(pool_set, 1)
            pool.wait_ge(pool_set, 14)
            pool.engine_nop().then_inc(consts, 1)

            pool.memset(pad_rows[:], 0).then_inc(pool_set, 1)
            pool.wait_ge(pool_set, 15)
            pool.memset(pad_rows[:, :, TARGET:TARGET + 1], NO_TARGET).then_inc(pads_set, 1)

            def rstd_of(g):
                pool.wait_ge(var2_ok, g + 1)
                root(rstd2[:, group(g)], var_eps2[:, group(g)], meanvar2[:, group(g), 1], minus_half[:, group(g)]).then_inc(rstd2_ok, 1)

            for step, g in ORDER:
                if step == RSTD2:
                    rstd_of(g)
                elif step == SEND and g < GROUPS - 1:
                    send(pool, g)
                elif step == SEND:
                    pool.wait_ge(pads_ok, 1)
                    pool.indirect_dma_start(rows_dram.rearrange("s (c one) -> (s c) one", one=1),
                                            bass.IndirectOffsetOnAxis(ap=pad_slot[:], axis=0),
                                            pad_rows[:].rearrange("p r c -> p (r c)"), None).then_inc(filled, 16)
                    send(pool, g)
            limit = pool.to_reg(SLOTS - 1)
            for t in range(N_TILES):
                for r in range(HALVES):
                    pool.wait_ge(y_ok, HALVES * t + r + 1)
                    pool.indirect_dma_start(results_dram, bass.IndirectOffsetOnAxis(ap=aims[:].bitcast(U32)[:, t, r, 0:1], axis=0),
                                            y_sb[:, t, r, :], None, bounds_check=limit,
                                            oob_is_err=False).then_inc(scattered, 16)

            q = chunks[POOL_CHUNK]
            pool.wait_ge(ld_res[POOL_CHUNK], 16)
            pool.tensor_tensor(out_sb[:, q, :], res[:, q, 0, :], neg_x1[:, q, :], ALU.subtract).then_inc(pool_summed, 1)
            pool.wait_ge(pool_summed, 1)
            pool.tensor_tensor(out_sb[:, q, :], out_sb[:, q, :], res[:, q, 1, :], ALU.add).then_inc(pool_out_ok, 1)

        @block.scalar
        def _(act):
            act.dma_start(wp[:], wpack).then_inc(ld_w, 16)
            act.wait_ge(ld_w, 16)
            act.activation(tanhs[:, 0:1], wp[:, GX:GX + 1], ACT.Tanh, scale=-1.0)
            act.activation(tanhs[:, 1:2], wp[:, GF:GF + 1], ACT.Tanh).then_inc(tanh_ok, 1)
            act.wait_ge(fused_ps, 1)
            act.activation(fused[:, 0:P], once[:, 0:P], ACT.Copy)
            act.wait_ge(tanh_ok, 1)
            act.activation(fused[:, P:2 * P], once[:, P:2 * P], ACT.Copy, scale=tanhs[:, 0:1])
            act.activation(fused[:, 2 * P:3 * P + 1], once[:, 2 * P:3 * P + 1], ACT.Copy).then_inc(fused_ok, 1)

            def copy_values(h):
                act.wait_ge(v_ps, h + 1)
                act.activation(v_sb[:, h * HALF:(h + 1) * HALF, 0:P], v_bank[h][:, :].rearrange("p (t d) -> p t d", d=P),
                               ACT.Copy).then_inc(v_ok, 1)

            def copy_nt(g):
                act.wait_ge(xnt_ps, g + 1)
                act.activation(xn_t[:, tokens(g)], xnt_bank[:, 0:SIZES[g] * P], ACT.Copy).then_inc(xnt_ok, 1)

            def copy_q(g):
                act.wait_ge(q_ps, g + 1)
                act.activation(q_t[:, tokens(g)], q_bank[:, 0:SIZES[g] * P], ACT.Identity,
                               bias=fused[:, 2 * P:2 * P + 1]).then_inc(q_ok, 1)

            def exp_scores(g):
                act.wait_ge(sub_ok, g + 1)
                if g == 0:
                    act.wait_ge(probs_zero, 1)
                for h in range(2):
                    half = slice(h * SEQ, (h + 1) * SEQ)
                    act.activation(probs[half, group(g), half], s_sub[half, group(g), :], ACT.Exp,
                                   scale=SCORE_SCALE).then_inc(prob_ok, 1)

            def copy_pt(g):
                act.wait_ge(pt_ps, g + 1)
                act.activation(p_t[:, tokens(g)], probs_bank[g % 2][:, 0:SIZES[g] * P], ACT.Copy).then_inc(pt_ok, 1)

            def centre(g):
                act.wait_ge(var2_ok, g + 1)
                for t in tiles_of(g):
                    m = act.activation(centred[:, t, :], neg_x1[:, t, :], ACT.Identity, bias=meanvar2[:, t, 0:1], scale=-1.0)
                m.then_inc(centred_ok, 1)

            def copy_ct(g):
                act.wait_ge(ct_ps, g + 1)
                act.activation(centred_t[:, tokens(g)], turn[g % 2][:, 0:SIZES[g] * P], ACT.Copy).then_inc(ct_ok, 1)

            def high_part(g):
                act.wait_ge(rstd2_ok, g + 1)
                for t in tiles_of(g):
                    act.activation(row_parts[:, t, 0, 0:P], centred[:, t, :], ACT.Copy,
                                   scale=rstd2[:, t:t + 1]).then_inc(hi_ok, 1)

            def second_rows(g):
                act.wait_ge(lo_ok, g + 1)
                act.activation(row_parts[:, group(g), 1, 0:2 * P], row_parts[:, group(g), 0, 0:2 * P], ACT.Copy).then_inc(twice_ok, 1)

            def exp_logits(g):
                act.wait_ge(shift_ok, g + 1)
                act.activation(exps[:, group(g), :], shifted[:, group(g), :], ACT.Exp).then_inc(exps_ok, 1)

            def weights_hi(to, at, loaded_all, made, i):
                act.wait_ge(loaded_all, 16)
                q = experts_of(i)
                act.activation(to[:, q], at[:, q], ACT.Copy, scale=WSCALE).then_inc(made, 1)

            for step, g in ORDER:
                if step == COPY_VALUES:
                    copy_values(g)
                elif step == COPY_NORM_T:
                    copy_nt(g)
                elif step == COPY_QUERIES:
                    copy_q(g)
                elif step == EXPONENT:
                    exp_scores(g)
                elif step == COPY_PROBS_T:
                    copy_pt(g)
                elif step == CENTRE:
                    centre(g)
                elif step == COPY_CENTRED_T:
                    copy_ct(g)
                elif step == HIGH:
                    high_part(g)
                elif step == EXP_LOGITS:
                    exp_logits(g)
                elif step == TWICE:
                    second_rows(g)
                elif step == W1_HIGH:
                    weights_hi(w1_hi, w1_sb, ld_w1, w1hi_ok, g)
                elif step == W2_HIGH:
                    weights_hi(w2_hi, w2_sb, ld_w2, w2hi_ok, g)

            b1 = wp[:, B1:B1 + EXPERTS * BLOCKS].rearrange("p (e b) -> p e b", b=BLOCKS)

            act.activation(gelu_first[:], tanhs[:], ACT.Gelu_apprx_tanh)
            act.wait_ge(table_ok, 1)
            experts = [act.value_load(tile_experts[0:1, t:t + 1], min_val=0, max_val=EXPERTS - 1) for t in range(N_TILES)]

            def high_parts(t, i):
                act.wait_ge(hid_ok, BLOCKS * t + 2 * i + 2)
                act.activation(hid_hi[:, t % 2, 2 * i:2 * i + 2, :], hid[:, t % 2, 2 * i:2 * i + 2, :], ACT.Copy).then_inc(hid_hi_ok, 1)

            for t in range(N_TILES):
                if t >= 2:
                    act.wait_ge(y_in_ps, t - 1)
                for b in range(BLOCKS):
                    if b % 2 == 0:
                        act.wait_ge(hid_in_ps, 2 * t + b // 2 + 1)
                    psum = hid_ps[t % 2][b // 2][:, b % 2 * SLOT_TILE:(b % 2 + 1) * SLOT_TILE]
                    act.activation(hid[:, t % 2, b, :], psum, ACT.Gelu_apprx_tanh, bias=b1[:, bass.ds(experts[t], 1), b:b + 1],
                                   scale=1.0 / WSCALE).then_inc(hid_ok, 1)
                    if b == 2:
                        high_parts(t, 0)
                high_parts(t, 1)

        @block.tensor
        def _(pe):
            def keep_clock(to, times):
                for _ in range(times):
                    pe.matmul(to, ones[:], ones[:, None, :].to_broadcast((P, 4, P)), start=True, stop=True)

            pe.wait_ge(ones_ok, 1)
            keep_clock(v_bank[0][:, :], CLOCK_START)
            pe.wait_ge(ld_w, 16)
            pe.wait_ge(dve_set, 1)
            ps = once
            pe.matmul(ps[:, 0:P], wp[:, WQ:WQ + P], wp[:, WK:WK + P], start=True, stop=True)
            pe.matmul(ps[:, P:2 * P], wp[:, WV:WV + P], wp[:, WOT:WOT + P], start=True, stop=True)
            pe.matmul(ps[:, 2 * P:2 * P + 1], wp[:, WK:WK + P], wp[:, BQ:BQ + 1], start=True, stop=True)
            pe.matmul(ps[:, 2 * P + 1:3 * P + 1], out_bias[:], wp[:, WOT:WOT + P], start=True, stop=True).then_inc(fused_ps, 1)

            def values(h):
                if h == 0:
                    pe.wait_ge(ld_ctx, 16)
                    pe.wait_ge(fused_ok, 1)
                for j in range(HALF):
                    t = h * HALF + j
                    mm = pe.matmul(v_bank[h][:, j * P:(j + 1) * P], ctx_sb[:, t * P:(t + 1) * P], fused[:, P:2 * P],
                                   start=True, stop=True)
                mm.then_inc(v_ps, 1)

            def norm_t(g):
                pe.wait_ge(xn_ok, STARTS[g + 1])
                if g:
                    pe.wait_ge(xnt_ok, g)
                for j in range(SIZES[g]):
                    mm = pe.transpose(xnt_bank[:, j * P:(j + 1) * P], xn[:, STARTS[g] + j, :], ident[:])
                mm.then_inc(xnt_ps, 1)

            def queries(g):
                pe.wait_ge(xnt_ok, g + 1)
                if g == 0:
                    pe.wait_ge(fused_ok, 1)
                if g:
                    pe.wait_ge(q_ok, g)
                pe.matmul(q_bank[:, 0:SIZES[g] * P], fused[:, 0:P], xn_t[:, tokens(g)],
                          start=True, stop=True).then_inc(q_ps, 1)

            def scores(g):
                pe.wait_ge(q_ok, g + 1)
                if g >= 2:
                    pe.wait_ge(var2_ok, g - 1)
                for j in range(SIZES[g]):
                    for h in range(2):
                        at = (STARTS[g] + j) * P + h * SEQ
                        mm = pe.matmul(score[g % 2][h * SEQ:(h + 1) * SEQ, j * SEQ:(j + 1) * SEQ],
                                       q_t[:, at:at + SEQ], ctx_sb[:, at:at + SEQ],
                                       start=True, stop=True)
                mm.then_inc(s_ps, 1)

            def probs_t(g):
                pe.wait_ge(prob_ok, 2 * (g + 1))
                if g >= 2:
                    pe.wait_ge(pt_ok, g - 1)
                for j in range(SIZES[g]):
                    mm = pe.transpose(probs_bank[g % 2][:, j * P:(j + 1) * P], probs[:, STARTS[g] + j, :], ident[:])
                mm.then_inc(pt_ps, 1)

            def attend(g):
                pe.wait_ge(pt_ok, g + 1)
                if g == 0:
                    pe.wait_ge(v_ones, 1)
                if g < 2:
                    pe.wait_ge(v_ok, g + 1)
                for j in range(SIZES[g]):
                    mm = pe.matmul(score[g % 2][:, j * (P + 1):(j + 1) * (P + 1)], p_t[:, (STARTS[g] + j) * P:(STARTS[g] + j + 1) * P],
                                   v_sb[:, STARTS[g] + j, :], start=True, stop=True)
                mm.then_inc(o_ps, 1)

            def centred_turn(g):
                pe.wait_ge(centred_ok, g + 1)
                if g >= 2:
                    pe.wait_ge(group_done, g - 1)
                for j in range(SIZES[g]):
                    mm = pe.transpose(turn[g % 2][:, j * P:(j + 1) * P], centred[:, STARTS[g] + j, :], ident[:])
                mm.then_inc(ct_ps, 1)

            def route(g):
                pe.wait_ge(ct_ok, g + 1)
                for j in range(SIZES[g]):
                    at = LOGIT + j * EXPERTS
                    mm = pe.matmul(turn[g % 2][:, at:at + EXPERTS], centred_t[:, (STARTS[g] + j) * P:(STARTS[g] + j + 1) * P],
                                   wp[:, GATEW:GATEW + EXPERTS], start=True, stop=True)
                mm.then_inc(logit_ps, 1)

            def ranks(g):
                pe.wait_ge(chosen_ok, g + 1)
                if g == 0:
                    pe.wait_ge(consts, 1)
                for j in range(SIZES[g]):
                    t = STARTS[g] + j
                    at = RANK + j * EXPERTS
                    mm = pe.matmul(turn[g % 2][:, at:at + EXPERTS], before[:], chosen[:, t, :], start=True, stop=t == 0)
                    for u in range(t):
                        mm = pe.matmul(turn[g % 2][:, at:at + EXPERTS], ones[:], chosen[:, u, :], start=False, stop=u == t - 1)
                mm.then_inc(rank_ps, 1)

            pe.wait_ge(ident_ok, 1)
            for step, g in ORDER:
                if step == VALUES:
                    values(g)
                elif step == NORM_T:
                    norm_t(g)
                elif step == QUERIES:
                    queries(g)
                elif step == SCORES:
                    scores(g)
                elif step == PROBS_T:
                    probs_t(g)
                elif step == ATTEND:
                    attend(g)
                elif step == CENTRED_T:
                    centred_turn(g)
                elif step == ROUTE:
                    route(g)
                elif step == RANKS:
                    ranks(g)
            for t in range(TILES):
                mm = pe.matmul(xnt_bank[:, COUNT:COUNT + EXPERTS], ones[:], chosen[:, t, :],
                               start=t == 0, stop=t == TILES - 1)
            mm.then_inc(count_ps, 1)

            def expert_of(t):
                return pe.value_load(tile_experts[0:1, t:t + 1], min_val=0, max_val=EXPERTS - 1)

            def turn_rows(t):
                s = t % 2
                buffer = t % ROW_BUFFERS
                pe.wait_ge(loaded[buffer], 16 * (t // ROW_BUFFERS + 1))
                if t >= 2:
                    pe.wait_ge(xs_ok, t - 1)
                to = xs_ps[s][:, :].bitcast(F16)
                for r in range(HALVES):
                    pe.transpose(to[:, r * P:(r + 1) * P], in_parts[:, buffer, r, 0:P], ident16[:])
                for r in range(HALVES):
                    mm = pe.transpose(to[:, SLOT_TILE + r * P:SLOT_TILE + (r + 1) * P], in_parts[:, buffer, r, P:2 * P], ident16[:])
                mm.then_inc(xs_in_ps, 1)

            def hidden(t, e):
                s = t % 2
                pe.wait_ge(xs_ok, t + 1)
                if t >= 2:
                    pe.wait_ge(hid_ok, BLOCKS * (t - 1))
                hi, lo = xs_t[:, s, 0, :], xs_t[:, s, 1, :]
                for b in range(BLOCKS):
                    to = hid_ps[s][b // 2][:, b % 2 * SLOT_TILE:(b % 2 + 1) * SLOT_TILE]
                    pe.matmul(to, w1_hi[:, bass.ds(e, 1), b * P:(b + 1) * P], hi, start=True, stop=False)
                    pe.matmul(to, w1_hi[:, bass.ds(e, 1), b * P:(b + 1) * P], lo, start=False, stop=False)
                    mm = pe.matmul(to, w1_lo[:, bass.ds(e, 1), b * P:(b + 1) * P], hi, start=False, stop=True)
                    if b % 2:
                        mm.then_inc(hid_in_ps, 1)

            def output(t, e):
                s = t % 2
                if t:
                    pe.wait_ge(y_ok, HALVES * t)
                for r in range(HALVES):
                    pe.matmul(y_ps[r][:, 0:P], out_sel[:], b2_16[:, bass.ds(e, 1), :], start=True, stop=False)
                for b in range(BLOCKS):
                    if b % 2 == 0:
                        pe.wait_ge(hid_hi_ok, 2 * t + b // 2 + 1)
                    for r in range(HALVES):
                        pe.matmul(y_ps[r][:, 0:P], hid_hi[:, s, b, r * P:(r + 1) * P], w2_lo[:, bass.ds(e, 1), b * P:(b + 1) * P],
                                  start=False, stop=False)
                for b in range(BLOCKS):
                    if b % 2 == 0:
                        pe.wait_ge(hid_lo_ok, 2 * t + b // 2 + 1)
                    for r in range(HALVES):
                        pe.matmul(y_ps[r][:, 0:P], hid_hi[:, s, b, r * P:(r + 1) * P], w2_hi[:, bass.ds(e, 1), b * P:(b + 1) * P],
                                  start=False, stop=False)
                        mm = pe.matmul(y_ps[r][:, 0:P], hid_lo[:, s, b, r * P:(r + 1) * P], w2_hi[:, bass.ds(e, 1), b * P:(b + 1) * P],
                                       start=False, stop=b == BLOCKS - 1)
                mm.then_inc(y_in_ps, 1)

            pe.wait_ge(row_ok, GROUPS)
            pe.wait_ge(table_ok, 1)
            experts = [expert_of(t) for t in range(AHEAD)]
            keep_clock(y_ps[0][:, :], CLOCK_ROWS)
            turn_rows(0)
            pe.wait_ge(w1_ok, PARTS)
            for t in range(N_TILES):
                if t + 1 < N_TILES:
                    turn_rows(t + 1)
                hidden(t, experts[t])
                if len(experts) < N_TILES:
                    experts.append(expert_of(len(experts)))
                if t == 1:
                    pe.wait_ge(w2_ok, PARTS)
                    pe.wait_ge(b2_ok, 1)
                if t:
                    output(t - 1, experts[t - 1])
            output(N_TILES - 1, experts[N_TILES - 1])

        @block.vector
        def _(v):
            done = 0

            def then(instruction):
                nonlocal done
                instruction.then_inc(dve, 1)
                done += 1
                return done

            v.memset(b2_in[:], 0.0).then_inc(zeroed, 1)
            v.memset(ones[:], 1.0).then_inc(ones_ok, 1)
            v.memset(v_sb[:, :, P:P + 1], 1.0).then_inc(v_ones, 1)
            then(v.memset(b2_16[:], 0.0))
            v.wait_ge(ld_w, 16)
            v.tensor_copy(out_bias[:], wp[:, BV:BV + 1].to_broadcast((P, P))).then_inc(dve_set, 1)

            def normalise(i):
                v.wait_ge(rstd_ok, i + 1)
                for t in range(*PIECES[i]):
                    v.tensor_scalar(xn[:, t, :], x_sb[:, t, :], meanvar[:, t, 0:1], rstd[:, t:t + 1],
                                    ALU.subtract, ALU.mult).then_inc(xn_ok, 1)

            for i, (a, b) in enumerate(PIECES):
                tiles = range(a, b)
                v.wait_ge(ld_x[i], 16)
                for t in tiles:
                    n = then(v.bn_stats(stats[:, t, :], x_sb[:, t, :]))
                v.wait_ge(dve, n)
                for t in tiles:
                    m = v.bn_aggr(meanvar[:, t, :], stats[:, t, :])
                m.then_inc(var_ok, 1)
                if i:
                    normalise(i - 1)
            v.wait_ge(fused_ok, 1)
            n = then(v.tensor_tensor(out_bias[:], fused[:, 2 * P + 1:3 * P + 1], wp[:, BO:BO + P], ALU.add))
            v.wait_ge(dve, n)
            v.wait_ge(tanh_ok, 1)
            then(v.tensor_scalar(gate_scale[:], tanhs[:, 1:2], 1.0 / WSCALE, None, ALU.mult))
            v.tensor_scalar(out_bias[:], out_bias[:], tanhs[:, 0:1], None, ALU.mult).then_inc(bias_ok, 1)
            normalise(len(PIECES) - 1)
            def biases():
                v.wait_ge(ld_b, 32)
                n = then(v.tensor_scalar(b2_hi[:], b2_in[:], WSCALE, None, ALU.mult))
                v.wait_ge(dve, n)
                parts = b2_16[:].rearrange("p e f -> p (e f)")
                v.scalar_tensor_tensor(parts[32:33, :], b2_in[32:33, :], WSCALE, b2_hi[32:33, :], ALU.mult, ALU.subtract)
                v.tensor_copy(parts[0:1, :], b2_hi[0:1, :]).then_inc(b2_ok, 1)

            def numbers():
                v.wait_ge(iotas, 6)
                then(v.tensor_copy(region[:], region_i[:]))
                then(v.tensor_copy(tile_no[:], tile_i[:]))
                then(v.tensor_copy(edge[:], edge_i[:]))
                then(v.tensor_copy(run_from[:], run_i[:]))
                n = then(v.tensor_copy(rows[:, :, :, TARGET], target[:]))
                v.wait_ge(dve, n)

            def score_max(g):
                s = score[g % 2][:, 0:SIZES[g] * SEQ].rearrange("p (j s) -> p j s", j=SIZES[g])
                v.wait_ge(s_ps, g + 1)
                n = then(v.tensor_reduce(s_max[:, group(g)], s, AX_X, ALU.max))
                v.wait_ge(dve, n)
                v.tensor_tensor(s_sub[:, group(g), :], s, s_max[:, group(g), None].to_broadcast((P, SIZES[g], SEQ)),
                                ALU.subtract).then_inc(sub_ok, 1)

            def residual(g):
                attended = score[g % 2][:, 0:SIZES[g] * (P + 1)].rearrange("p (j c) -> p j c", j=SIZES[g])
                v.wait_ge(o_ps, g + 1)
                n = then(v.reciprocal(rden[:, group(g)], attended[:, :, P]))
                v.wait_ge(dve, n)
                v.wait_ge(xbias_ok, 1)
                for j in range(SIZES[g]):
                    t = STARTS[g] + j
                    n = then(v.scalar_tensor_tensor(neg_x1[:, t, :], attended[:, j, 0:P], rden[:, t:t + 1],
                                                    x_bias[:, t, :], ALU.mult, ALU.add))
                v.wait_ge(dve, n)
                for t in tiles_of(g):
                    n = then(v.bn_stats(stats2[:, t, :], neg_x1[:, t, :]))
                v.wait_ge(dve, n)
                for t in tiles_of(g):
                    m = v.bn_aggr(meanvar2[:, t, :], stats2[:, t, :])
                m.then_inc(var2_ok, 1)

            def choose(g):
                v.wait_ge(logit_ps, g + 1)
                v.wait_ge(rstd2_ok, g + 1)
                n = then(v.tensor_tensor(logits[:, group(g), :], turn[g % 2][:, LOGIT:LOGIT + SIZES[g] * EXPERTS].rearrange(
                    "p (j e) -> p j e", j=SIZES[g]), rstd2[:, group(g), None].to_broadcast((P, SIZES[g], EXPERTS)), ALU.mult))
                v.wait_ge(dve, n)
                for t in tiles_of(g):
                    n = then(v.max(sorted_l[:, t, :], logits[:, t, :]))
                v.wait_ge(dve, n)
                for t in tiles_of(g):
                    n = then(v.max_index(index[:, t, :], sorted_l[:, t, :], logits[:, t, :]))
                v.tensor_tensor(shifted[:, group(g), :], sorted_l[:, group(g), :],
                                sorted_l[:, group(g), 0:1].to_broadcast((P, SIZES[g], EXPERTS)), ALU.subtract).then_inc(shift_ok, 1)
                v.wait_ge(dve, n)
                n = then(v.tensor_tensor(choice[:, group(g), :, :], iota_i[:, None, None, :].to_broadcast((P, SIZES[g], TOP_K, EXPERTS)),
                                         index[:, group(g), 0:TOP_K, None].to_broadcast((P, SIZES[g], TOP_K, EXPERTS)), ALU.is_equal))
                v.wait_ge(dve, n)
                v.tensor_tensor(chosen[:, group(g), :], choice[:, group(g), 0, :], choice[:, group(g), 1, :],
                                ALU.add).then_inc(chosen_ok, 1)

            def low_parts(g):
                for t in tiles_of(g):
                    v.wait_ge(hi_ok, t + 1)
                    m = v.scalar_tensor_tensor(row_parts[:, t, 0, P:2 * P], centred[:, t, :], rstd2[:, t:t + 1],
                                               row_parts[:, t, 0, 0:P], ALU.mult, ALU.subtract)
                m.then_inc(lo_ok, 1)

            def fill_rows_of(g):
                v.wait_ge(exps_ok, g + 1)
                n = then(v.tensor_reduce(exp_sum[:, group(g)], exps[:, group(g), :], AX_X, ALU.add))
                v.wait_ge(dve, n)
                n = then(v.reciprocal(exp_rec[:, group(g)], exp_sum[:, group(g)]))
                v.wait_ge(dve, n)
                then(v.scalar_tensor_tensor(rows[:].bitcast(F32)[:, group(g), :, GATE], exps[:, group(g), 0:TOP_K], gate_scale[:, 0:1],
                                            exp_rec[:, group(g), None].to_broadcast((P, SIZES[g], TOP_K)), ALU.mult, ALU.mult))
                v.wait_ge(rank_ps, g + 1)
                v.tensor_tensor(place[:, group(g), :], turn[g % 2][:, RANK:RANK + SIZES[g] * EXPERTS].rearrange("p (j e) -> p j e", j=SIZES[g]),
                                region[:, None, :].to_broadcast((P, SIZES[g], EXPERTS)), ALU.add).then_inc(group_done, 1)
                v.wait_ge(group_done, g + 1)
                n = then(v.tensor_tensor(place_k[:, group(g), :, :], choice[:, group(g), :, :],
                                         place[:, group(g), None, :].to_broadcast((P, SIZES[g], TOP_K, EXPERTS)), ALU.mult))
                v.wait_ge(dve, n)
                n = then(v.tensor_reduce(slot_f[:, group(g), :], place_k[:, group(g), :, :], AX_X, ALU.add))
                v.wait_ge(dve, n)
                v.tensor_copy(slot[:, TOP_K * STARTS[g]:TOP_K * STARTS[g + 1]],
                              slot_f[:, group(g), :].rearrange("p t k -> p (t k)")).then_inc(row_ok, 1)

            def weights_lo(to, at, hi, hi_made, made_lo, i):
                q = experts_of(i)
                v.wait_ge(hi_made, i + 1)
                v.scalar_tensor_tensor(to[:, q, :], at[:, q, :], WSCALE, hi[:, q, :], ALU.mult, ALU.subtract).then_inc(made_lo, 1)

            for step, g in ORDER:
                if step == BIASES:
                    biases()
                elif step == NUMBERS:
                    numbers()
                elif step == MAXIMUM:
                    score_max(g)
                elif step == RESIDUAL:
                    residual(g)
                elif step == CHOOSE:
                    choose(g)
                elif step == LOW:
                    low_parts(g)
                elif step == FILL:
                    fill_rows_of(g)
                elif step == W1_LOW and PART_TIMES[2][g] < TABLE:
                    weights_lo(w1_lo, w1_sb, w1_hi, w1hi_ok, w1_ok, g)
                elif step == W2_LOW and PART_TIMES[3][g] < TABLE:
                    weights_lo(w2_lo, w2_sb, w2_hi, w2hi_ok, w2_ok, g)

            v.wait_ge(count_ps, 1)
            then(v.tensor_copy(counts[:], xnt_bank[0:1, COUNT:COUNT + EXPERTS]))
            n = then(v.tensor_tensor(run_row[:], xnt_bank[:, COUNT:COUNT + EXPERTS], run_from[:], ALU.add))
            v.wait_ge(dve, n)
            then(v.tensor_tensor(run_word[:], run_row[:], run_sel[:], ALU.mult))
            n = then(v.tensor_tensor(over[:], counts[:, :, None].to_broadcast((1, EXPERTS, EDGES)), edge[:], ALU.is_gt))
            v.wait_ge(dve, n)
            then(v.tensor_reduce(pad_at[:], run_word[:], AX_X, ALU.add))
            n = then(v.tensor_reduce(n_tiles[:], over[:], AX_X, ALU.add))
            v.wait_ge(dve, n)
            v.tensor_copy(pad_slot[:], pad_at[:]).then_inc(pads_ok, 1)
            n = then(v.tensor_tensor(upto_n[:], upto[:], n_tiles[:, None, :].to_broadcast((1, EXPERTS, EXPERTS)), ALU.mult))
            v.wait_ge(dve, n)
            n = then(v.tensor_reduce(ends[:], upto_n[:], AX_X, ALU.add))
            v.wait_ge(dve, n)
            n = then(v.tensor_tensor(past[:], tile_no[:], ends[:, None, :].to_broadcast((1, N_TILES, EXPERTS)), ALU.is_ge))
            v.wait_ge(dve, n)
            then(v.tensor_reduce(tile_e[:], past[:], AX_X, ALU.add))
            n = then(v.tensor_tensor(past_n[:], past[:], n_tiles[:, None, :].to_broadcast((1, N_TILES, EXPERTS)), ALU.mult))
            v.wait_ge(dve, n)
            n = then(v.tensor_reduce(tile_base[:], past_n[:], AX_X, ALU.add))
            v.wait_ge(dve, n)
            then(v.tensor_scalar(tile_experts[:], tile_e[:], float(EXPERTS - 1), None, ALU.min))
            n = then(v.tensor_tensor(tile_row[:], tile_no[:, :, 0], tile_base[:], ALU.subtract))
            v.wait_ge(dve, n)
            n = then(v.tensor_scalar(tile_row2[:], tile_e[:], float(REGION // SLOT_TILE), None, ALU.mult))
            v.wait_ge(dve, n)
            n = then(v.tensor_tensor(tile_base[:], tile_row[:], tile_row2[:], ALU.add))
            v.wait_ge(dve, n)
            v.tensor_scalar(tile_rows[:], tile_base[:], float(SLOT_TILE), float(PAD_ROW), ALU.mult, ALU.min).then_inc(table_ok, 1)

            for step, g in ORDER:
                if step == W1_LOW and PART_TIMES[2][g] >= TABLE:
                    weights_lo(w1_lo, w1_sb, w1_hi, w1hi_ok, w1_ok, g)
                elif step == W2_LOW and PART_TIMES[3][g] >= TABLE and g < PARTS - 1:
                    weights_lo(w2_lo, w2_sb, w2_hi, w2hi_ok, w2_ok, g)

            def copy_rows(t, s, first=False):
                v.wait_ge(xs_in_ps, t + 1)
                if not first:
                    v.wait_ge(hid_in_ps, t - 1)
                v.tensor_copy(xs_t[:, s, :, :], xs_ps[s][:, :].bitcast(F16)[:, 0:2 * SLOT_TILE].rearrange("p (c s) -> p c s", c=2)).then_inc(xs_ok, 1)
                v.tensor_copy(aims[:, t, :, :], in_rows[:, t % ROW_BUFFERS, :, TARGET:GATE + 1]).then_inc(row_read, 1)

            def low_part(t, s, first=False):
                if not first:
                    v.wait_ge(y_in_ps, t - 1)
                for i in range(2):
                    v.wait_ge(hid_hi_ok, 2 * t + i + 1)
                    b = slice(2 * i, 2 * i + 2)
                    v.tensor_tensor(hid_lo[:, s, b, :], hid[:, s, b, :], hid_hi[:, s, b, :], ALU.subtract).then_inc(hid_lo_ok, 1)

            def gated(t, s):
                v.wait_ge(y_in_ps, t + 1)
                v.wait_ge(row_read, t + 1)
                for r in range(HALVES):
                    v.tensor_scalar(y_sb[:, t, r, :], y_ps[r][:, 0:P], aims[:].bitcast(F32)[:, t, r, 1:2], None,
                                    ALU.mult).then_inc(y_ok, 1)

            copy_rows(0, 0, True)
            copy_rows(1, 1, True)
            weights_lo(w2_lo, w2_sb, w2_hi, w2hi_ok, w2_ok, PARTS - 1)
            for t in range(N_TILES):
                low_part(t, t % 2, t < 2)
                if t + 2 < N_TILES:
                    copy_rows(t + 2, t % 2)
                gated(t, t % 2)

            for i, q in enumerate(chunks):
                if i != POOL_CHUNK:
                    v.wait_ge(ld_res[i], 16)
                    n = then(v.tensor_tensor(out_sb[:, q, :], res[:, q, 0, :], neg_x1[:, q, :], ALU.subtract))
                    v.wait_ge(dve, n)
                    v.tensor_tensor(out_sb[:, q, :], out_sb[:, q, :], res[:, q, 1, :], ALU.add).then_inc(out_ok, 1)


def kernel(**inputs):
    import numpy as np
    import concourse.bacc as bacc
    from concourse.bass_utils import run_bass_kernel_spmd

    a = {name: np.asarray(value) for name, value in inputs.items()}
    wide = [a["L0_xattn_Wq"], a["L0_xattn_Wk"], a["L0_xattn_Wv"], a["L0_xattn_Wo"].T, a["L0_ffn_gate_w"].T,
            a["L0_xattn_bq"][:, None], a["L0_xattn_bv"][:, None],
            np.broadcast_to(a["L0_xattn_bo"][None, :], (P, P)),
            np.broadcast_to(a["g_xattn"][None, :], (P, 1)), np.broadcast_to(a["g_ffn"][None, :], (P, 1)),
            a["L0_ffn_b1"].reshape(EXPERTS * BLOCKS, P).T]
    arrays = {
        "x": a["x"].reshape(TOKENS, P),
        "ctx_t": a["ctx_1024"].reshape(TOKENS, P).T,
        "wpack": np.concatenate(wide, axis=1),
        "b2": a["L0_ffn_b2"].reshape(1, EXPERTS * P),
        "w1": a["L0_ffn_w1"].transpose(2, 1, 0),
        "w2": a["L0_ffn_w2"].reshape(P, EXPERTS, BLOCKS, P).transpose(3, 1, 2, 0).reshape(P, EXPERTS, FF),
    }
    arrays = {f"in_{name}": np.ascontiguousarray(value) for name, value in arrays.items()}

    nc = bacc.Bacc("TRN2", target_bir_lowering=False, num_devices=1)
    args = [nc.dram_tensor(name, value.shape, mybir.dt.from_np(value.dtype), kind="ExternalInput").ap()
            for name, value in arrays.items()]
    out = nc.dram_tensor("out", (TOKENS, P), F32, kind="ExternalOutput").ap()
    gated_block(nc, *args, out)
    result = run_bass_kernel_spmd(nc, [arrays], core_ids=[0])
    return result.results[0]["out"].reshape(BATCH, SEQ, P)
```
